# Optimizing a Trainium2 kernel written in Bass

```python
import numpy as np
import jax
import jax.numpy as jnp

def _softmax(x, axis=-1):
    return jax.nn.softmax(x, axis=axis)
def _gelu(x):
    return jax.nn.gelu(x, approximate=True)
def _silu(x):
    return jax.nn.silu(x)
def _sigmoid(x):
    return jax.nn.sigmoid(x)
def _layernorm(x, axis=-1, eps=1e-5):
    m = jnp.mean(x, axis=axis, keepdims=True)
    v = jnp.var(x, axis=axis, keepdims=True)
    return (x - m) / jnp.sqrt(v + eps)
def _scatter_add(tgt, idx, src, axis=0):
    return tgt.at[idx].add(src)
def _segment_sum(src, seg, n):
    return jax.ops.segment_sum(src, seg, n)

kernel_name = 'mk_conv_seq_d1_conv_nchw96_202920'

def setup_inputs(seed: int = 0):
    np.random.seed(seed)
    _w = jnp.asarray
    def _rec_inputs():
        import jax
        import jax.numpy as jnp
        _gk = jax.random.key(seed)
        x = -0.0006872 + 1.001 * jax.random.normal(jax.random.fold_in(_gk, 1), (8, 96, 56, 56), jnp.float32)
        return x
    x = _rec_inputs()
    def _L0_conv_setup():
        import jax, jax.numpy as jnp
        import numpy as np
        from jax import lax
        EPS = 1e-12
        N_ITER = 25
        PAD = 1
        GROUPS = 4

        def conv2d(x, w, padding, groups):
            return lax.conv_general_dilated(x, w, (1, 1), ((padding, padding), (padding, padding)), dimension_numbers=('NCHW', 'OIHW', 'NCHW'), feature_group_count=groups)

        def conv_transpose2d(h, w, padding, groups):
            O, Ig, kh, kw = w.shape
            I = Ig * groups
            wt = w.reshape(groups, O // groups, Ig, kh, kw).transpose(0, 2, 1, 3, 4)
            wt = wt.reshape(I, O // groups, kh, kw)[:, :, ::-1, ::-1]
            return conv2d(h, wt, kh - 1 - padding, groups)

        def nnmf_conv2d(x, weight, n_iterations=N_ITER, padding=PAD, groups=GROUPS, normalize_channels=True):
            w = jnp.abs(weight)
            w = w / (w.sum(axis=(1, 2, 3), keepdims=True) + EPS)
            x = x / (x.sum(axis=1, keepdims=True) + EPS)
            N, C, H, W = x.shape
            O = weight.shape[0]
            h0 = jnp.full((N, O, H, W), 1.0 / O, dtype=x.dtype)

            def body(i, h):
                recon = conv_transpose2d(h, w, padding, groups)
                ratio = x / (recon + EPS)
                h = h * conv2d(ratio, w, padding, groups)
                if normalize_channels:
                    h = h / (h.sum(axis=1, keepdims=True) + EPS)
                return h
            return lax.fori_loop(0, n_iterations, body, h0)

        def layernorm_cf(x, w, b, eps=1e-06):
            u = x.mean(axis=1, keepdims=True)
            s = jnp.mean((x - u) ** 2, axis=1, keepdims=True)
            xn = (x - u) * lax.rsqrt(s + eps)
            return w[None, :, None, None] * xn + b[None, :, None, None]

        def layernorm_last(x, w, b, eps=1e-05):
            u = x.mean(axis=-1, keepdims=True)
            s = jnp.mean((x - u) ** 2, axis=-1, keepdims=True)
            return (x - u) * lax.rsqrt(s + eps) * w + b
        key = jax.random.key(seed)
        ks = jax.random.split(key, 8)
        C, Hd = (96, 384)
        x = jax.random.normal(ks[0], (8, C, 56, 56), dtype=jnp.float32)
        return {'x': x, 'ln1_w': jnp.ones((C,), jnp.float32), 'ln1_b': jnp.zeros((C,), jnp.float32), 'w_nnmf': jax.random.uniform(ks[1], (C, C // GROUPS, 3, 3), jnp.float32, 0.01, 1.0), 'ln2_w': jnp.ones((C,), jnp.float32), 'ln2_b': jnp.zeros((C,), jnp.float32), 'w1': jax.random.normal(ks[2], (C, Hd), jnp.float32) * 0.02, 'b1': jnp.zeros((Hd,), jnp.float32), 'w2': jax.random.normal(ks[3], (Hd, C), jnp.float32) * 0.02, 'b2': jnp.zeros((C,), jnp.float32)}
    _L0_conv_all = _L0_conv_setup()
    _L0_conv_in = {k: v for k, v in _L0_conv_all.items() if k in ('ln1_w', 'ln1_b', 'w_nnmf', 'ln2_w', 'ln2_b', 'w1', 'b1', 'w2', 'b2', )}
    del _L0_conv_all

    return {
        "x": x,
        "L0_conv_ln1_w": _L0_conv_in["ln1_w"],
        "L0_conv_ln1_b": _L0_conv_in["ln1_b"],
        "L0_conv_w_nnmf": _L0_conv_in["w_nnmf"],
        "L0_conv_ln2_w": _L0_conv_in["ln2_w"],
        "L0_conv_ln2_b": _L0_conv_in["ln2_b"],
        "L0_conv_w1": _L0_conv_in["w1"],
        "L0_conv_b1": _L0_conv_in["b1"],
        "L0_conv_w2": _L0_conv_in["w2"],
        "L0_conv_b2": _L0_conv_in["b2"],
    }

def reference(x, L0_conv_ln1_w, L0_conv_ln1_b, L0_conv_w_nnmf, L0_conv_ln2_w, L0_conv_ln2_b, L0_conv_w1, L0_conv_b1, L0_conv_w2, L0_conv_b2):
    import jax
    import jax.numpy as jnp
    def _L0_conv_ref(x, ln1_w, ln1_b, w_nnmf, ln2_w, ln2_b, w1, b1, w2, b2):
        import jax, jax.numpy as jnp
        import numpy as np
        from jax import lax
        EPS = 1e-12
        N_ITER = 25
        PAD = 1
        GROUPS = 4

        def conv2d(x, w, padding, groups):
            return lax.conv_general_dilated(x, w, (1, 1), ((padding, padding), (padding, padding)), dimension_numbers=('NCHW', 'OIHW', 'NCHW'), feature_group_count=groups)

        def conv_transpose2d(h, w, padding, groups):
            O, Ig, kh, kw = w.shape
            I = Ig * groups
            wt = w.reshape(groups, O // groups, Ig, kh, kw).transpose(0, 2, 1, 3, 4)
            wt = wt.reshape(I, O // groups, kh, kw)[:, :, ::-1, ::-1]
            return conv2d(h, wt, kh - 1 - padding, groups)

        def nnmf_conv2d(x, weight, n_iterations=N_ITER, padding=PAD, groups=GROUPS, normalize_channels=True):
            w = jnp.abs(weight)
            w = w / (w.sum(axis=(1, 2, 3), keepdims=True) + EPS)
            x = x / (x.sum(axis=1, keepdims=True) + EPS)
            N, C, H, W = x.shape
            O = weight.shape[0]
            h0 = jnp.full((N, O, H, W), 1.0 / O, dtype=x.dtype)

            def body(i, h):
                recon = conv_transpose2d(h, w, padding, groups)
                ratio = x / (recon + EPS)
                h = h * conv2d(ratio, w, padding, groups)
                if normalize_channels:
                    h = h / (h.sum(axis=1, keepdims=True) + EPS)
                return h
            return lax.fori_loop(0, n_iterations, body, h0)

        def layernorm_cf(x, w, b, eps=1e-06):
            u = x.mean(axis=1, keepdims=True)
            s = jnp.mean((x - u) ** 2, axis=1, keepdims=True)
            xn = (x - u) * lax.rsqrt(s + eps)
            return w[None, :, None, None] * xn + b[None, :, None, None]

        def layernorm_last(x, w, b, eps=1e-05):
            u = x.mean(axis=-1, keepdims=True)
            s = jnp.mean((x - u) ** 2, axis=-1, keepdims=True)
            return (x - u) * lax.rsqrt(s + eps) * w + b
        x_norm = layernorm_cf(x, ln1_w, ln1_b)
        x = x + nnmf_conv2d(jax.nn.relu(x_norm), w_nnmf)
        xl = jnp.transpose(x, (0, 2, 3, 1))
        h = layernorm_last(xl, ln2_w, ln2_b)
        h = jax.nn.gelu(h @ w1 + b1, approximate=False) @ w2 + b2
        xl = xl + h
        return jnp.transpose(xl, (0, 3, 1, 2))

    def _gn(v, G=32, eps=1e-5):
        B_, C_, H_, W_ = v.shape
        g = v.reshape(B_, G, C_ // G, H_, W_)
        m = jnp.mean(g, axis=(2, 3, 4), keepdims=True)
        s = jnp.var(g, axis=(2, 3, 4), keepdims=True)
        return ((g - m) / jnp.sqrt(s + eps)).reshape(v.shape)

    def _ln_c(v, eps=1e-6):
        m = jnp.mean(v, axis=1, keepdims=True)
        s = jnp.var(v, axis=1, keepdims=True)
        return (v - m) / jnp.sqrt(s + eps)

    def _ln_t(v, eps=1e-5):
        m = jnp.mean(v, axis=-1, keepdims=True)
        s = jnp.var(v, axis=-1, keepdims=True)
        return (v - m) / jnp.sqrt(s + eps)

    def _to_tokens(v):
        B_, C_, H_, W_ = v.shape
        return v.reshape(B_, C_, H_ * W_).transpose(0, 2, 1)
    def _from_tokens(t, like):
        B_, C_, H_, W_ = like.shape
        return t.transpose(0, 2, 1).reshape(B_, C_, H_, W_)

    x = _L0_conv_ref(x, L0_conv_ln1_w, L0_conv_ln1_b, L0_conv_w_nnmf, L0_conv_ln2_w, L0_conv_ln2_b, L0_conv_w1, L0_conv_b1, L0_conv_w2, L0_conv_b2)
    return x


_drawn_inputs = setup_inputs


def setup_inputs(seed=0):
    import zlib

    import numpy as np

    out = dict(_drawn_inputs(seed))
    spreads = {'L0_conv_ln1_w': (1.0, 0.6),
     'L0_conv_ln1_b': (0.0, 0.8),
     'L0_conv_ln2_w': (1.0, 0.6),
     'L0_conv_ln2_b': (0.0, 0.8),
     'L0_conv_b1': (0.0, 0.39),
     'L0_conv_b2': (0.0, 0.1)}
    factors = {'L0_conv_w_nnmf': 3.089}
    for name, (base, spread) in spreads.items():
        noise = np.random.default_rng([zlib.crc32(name.encode()), seed]).standard_normal(out[name].shape)
        drawn = base * np.exp(spread * noise) if base else spread * noise
        out[name] = jnp.asarray(drawn.astype(out[name].dtype))
    for name, factor in factors.items():
        out[name] = (out[name] * factor).astype(out[name].dtype)
    return out
```

```python
import concourse.bass as bass
from concourse import mybir
from contextlib import ExitStack

N_IMG, C, H, W = 8, 96, 56, 56
GROUPS = 4
CG = C // GROUPS
HID = 384
N_ITER = 25
EPS = 1e-12
LN1_EPS = 1e-6
LN2_EPS = 1e-5
Q = 32
SLOTS = H // 4
WP = W + 2
HALF = SLOTS // 2
BANK = HALF * W
PLANE = SLOTS * W
BATCH = 2
N_BATCH = N_IMG // BATCH
PLANES = BATCH * GROUPS
PAIRS = 3

ORDER = ([("T", 0, 0), ("T", 0, 1), ("S", 1, 0), ("T", 0, 2), ("T", 0, 3)]
         + [("T", 1, g) for g in range(GROUPS)] + [("C", 0, g) for g in range(GROUPS)]
         + [("C", 1, 0), ("C", 1, 1), ("S", 0, 0), ("C", 1, 2), ("C", 1, 3)])
ITER_UNITS = len(ORDER)
assert ITER_UNITS % PAIRS == 0
HEAD_UNITS = 3 * BATCH
TAIL_UNITS = 1 + 2 * BATCH
assert HEAD_UNITS % PAIRS == 0


def plane_index(image, g):
    return image * GROUPS + g


def build_nnmf_block(nc, x, ln1_w, ln1_b, w_nnmf, ln2_w, ln2_b, w1, b1, w2, b2, out):
    f32 = mybir.dt.float32
    ALU = mybir.AluOpType
    ACT = mybir.ActivationFunctionType
    AX = mybir.AxisListType

    y_dram = nc.dram_tensor("y_scratch", (N_IMG, C, H, W), f32, kind="Internal").ap()
    n_dram = nc.dram_tensor("n_scratch", (N_IMG, C, H, W), f32, kind="Internal").ap()

    def row_quads(t):
        return t.rearrange("n (g c) (k j) w -> n g j c k w", g=GROUPS, j=4)

    x_q, y_q, n_q = row_quads(x), row_quads(y_dram), row_quads(n_dram)

    with ExitStack() as ctx:
        def sb(name, shape):
            return ctx.enter_context(nc.sbuf_tensor(name, shape, f32))

        def sem(name):
            return ctx.enter_context(nc.semaphore(name))

        xn = sb("xn", [128, BATCH, GROUPS, PLANE])
        xraw = sb("xraw", [128, BATCH, GROUPS, PLANE])
        h_even = sb("h_even", [128, BATCH, GROUPS, SLOTS, WP])
        h_odd = sb("h_odd", [128, BATCH, GROUPS, SLOTS + 1, WP])
        r_even = sb("r_even", [128, BATCH, GROUPS, SLOTS, WP])
        r_odd = sb("r_odd", [128, BATCH, GROUPS, SLOTS + 1, WP])
        seed = sb("seed", [128, 2, PLANE])
        prod = sb("prod", [128, 2, PLANE])
        xseed = sb("xseed", [128, 2, PLANE])
        usum = sb("usum", [128, BATCH, PLANE])
        upart = sb("upart", [128, PLANE])
        norm = sb("norm", [128, 3, PLANE])
        W_T, W_C = 0, 1
        wt = sb("wt", [128, 2, GROUPS, 3, 2, Q])
        negones = sb("negones", [128, 128])
        ln_par = sb("ln_par", [128, 4, GROUPS])
        w1_sb = sb("w1_sb", [C, HID])
        w2_sb = sb("w2_sb", [128, HID // 128, C])
        b1_sb = sb("b1_sb", [128, HID // 128])
        b2_sb = sb("b2_sb", [C, 1])
        eps_sb = sb("eps_sb", [128, 3])
        ps = ctx.enter_context(nc.psum_tensor("ps", [128, 8, 512], f32))

        w_raw = prod[:, 0, 0:CG * 9]
        w_abs = prod[:, 1, 0:CG * 9]
        w_nrm = seed[:, 0, 0:9 * Q]
        w_tr = seed[:, 1, 0:9 * Q]
        w_sum = norm[:, 0, 0:1]
        w_inv = norm[:, 1, 0:1]

        MT_ROWS = 8
        MT = MT_ROWS * W
        xn_flat = xn[:, :, :, :].rearrange("p a g c -> p (a g c)")
        HT = HID // 128

        def carve(start, parts, count):
            return xn_flat[0:parts, start:start + count * MT].rearrange("p (n c) -> p n c", n=count)

        m_n, m_y = carve(0, C, 2), carve(2 * MT, C, 2)
        m_hid, m_out = carve(4 * MT, 128, 2 * HT), carve((4 + 2 * HT) * MT, C, 2)

        def inner(buf, image, g):
            return buf[:, image, g, 0:SLOTS, 1:1 + W].rearrange("p (b s) w -> p b s w", b=2)

        def flat(ap):
            return ap.rearrange("p (b s w) -> p b s w", b=2, s=HALF)

        def pair(unit):
            p = unit % PAIRS
            return ps[:, 2 * p:2 * p + 2, 0:BANK].rearrange("p b (s w) -> p b s w", s=HALF)

        w_cleared = sem("w_cleared")
        ones_set = sem("ones_set")
        w_in = sem("w_in")
        params_in = sem("params_in")
        buffers_cleared = sem("buffers_cleared")
        weight_step = sem("weight_step")
        weights_ready = sem("weights_ready")
        xn_in = sem("xn_in")
        xraw_in = sem("xraw_in")
        y_stored = sem("y_stored")
        n_stored = sem("n_stored")
        ln_sum_done = sem("ln_sum_done")
        centered = sem("centered")
        squared = sem("squared")
        square_summed = sem("square_summed")
        scaled = sem("scaled")
        affine_done = sem("affine_done")
        x_ready = sem("x_ready")
        recon_done = sem("recon_done")
        conv_done = sem("conv_done")
        chan_done = sem("chan_done")
        log_done = sem("log_done")
        seed_ready = sem("seed_ready")
        norm_seed_ready = sem("norm_seed_ready")
        norm_step = sem("norm_step")
        xseed_ready = sem("xseed_ready")
        prod_done = sem("prod_done")
        ratio_ready = sem("ratio_ready")
        ratio_both = sem("ratio_both")
        u_ready = sem("u_ready")
        part_done = sem("part_done")
        usum_ready = sem("usum_ready")
        h_ready = sem("h_ready")
        h_both = sem("h_both")
        y_ready = sem("y_ready")
        mlp_n_in = [sem("mlp_n_in0"), sem("mlp_n_in1")]
        mlp_y_in = [sem("mlp_y_in0"), sem("mlp_y_in1")]
        hidden_done = sem("hidden_done")
        gelu_done = sem("gelu_done")
        mlp_done = sem("mlp_done")
        out_ready = sem("out_ready")
        out_stored = sem("out_stored")

        block = ctx.enter_context(nc.Block())

        PLANES_PB = N_ITER * PLANES
        HB_PB = GROUPS + PLANES_PB
        H_PB = PLANES_PB + GROUPS
        US_PB = 1 + N_ITER * BATCH
        CH_PB = N_ITER * BATCH + 1
        LNS = 2 * BATCH
        LN_PLANES_PB = LNS * GROUPS
        HEAD_SUMS = 2 * BATCH
        SUMS_PB = HEAD_SUMS + BATCH
        HEAD_LOGS = 2 * BATCH
        LOGS_IT = PLANES + BATCH
        LOGS_PB = HEAD_LOGS + N_ITER * LOGS_IT + 1 + BATCH
        NS_PB = HEAD_LOGS + N_ITER * BATCH + 1 + BATCH
        LN_STEPS, INV_STEPS = 5, 2
        HEAD_STEPS = BATCH * (LN_STEPS + INV_STEPS)
        STEPS_PB = HEAD_STEPS + N_ITER * BATCH * INV_STEPS + INV_STEPS + BATCH * LN_STEPS
        WEIGHT_STEPS = 6
        N_PARAM_DMA = 4 * 4 + 4
        LOAD = 16 * 4 * PLANES
        PRIMED, PRIMED_DMA = 1, 16
        TAIL = HEAD_UNITS + N_ITER * ITER_UNITS

        def batches(eng, body):
            with eng.Fori(0, N_BATCH - 1) as b:
                body(b, False)
            body(N_BATCH - 1, True)

        MLP_PAIRS, MLP_TILES = N_IMG // 2, H // MT_ROWS

        def mlp_loop(eng, body):
            with eng.Fori(0, MLP_PAIRS) as m:
                with eng.Fori(0, MLP_TILES) as t:
                    body(m, t, m * MLP_TILES + t)

        def mlp_tiles(t):
            return t.rearrange("(m e) c (t r) w -> m e t c r w", e=2, r=MT_ROWS)

        @block.sync
        def _(sp):
            sp.sem_inc(y_stored, PRIMED_DMA)
            sp.sem_inc(n_stored, PRIMED_DMA)
            sp.wait_ge(w_cleared, 1)
            for g in range(GROUPS):
                sp.dma_start(w_raw[Q * g:Q * g + CG, :],
                             w_nnmf[CG * g:CG * (g + 1)].rearrange("o i a b -> o (i a b)")).then_inc(w_in, 16)

            def load(dst, b, signal):
                for image in range(BATCH):
                    for g in range(GROUPS):
                        for j in range(4):
                            sp.dma_start(dst[Q * j:Q * j + CG, image, g, :].rearrange("p (k w) -> p k w", w=W),
                                         x_q[b * BATCH + image, g, j]).then_inc(signal, 16)

            def store(image, g, src, dst, b, signal):
                for j in range(4):
                    sp.dma_start(dst[b * BATCH + image, g, j], src(j)).then_inc(signal, 16)

            sp.wait_ge(buffers_cleared, 1)
            load(xn, 0, xn_in)
            sp.wait_ge(buffers_cleared, 2)
            for n, par in enumerate((ln1_w, ln1_b, ln2_w, ln2_b)):
                for j in range(4):
                    sp.dma_start(ln_par[Q * j:Q * j + CG, n, :], par.rearrange("(g c) -> c g", c=CG),
                                 allow_slow_non_contiguous=True).then_inc(params_in, 16)
            sp.dma_start(w1_sb[:, :], w1[:, :]).then_inc(params_in, 16)
            sp.dma_start(w2_sb[:, :, :], w2.rearrange("(t p) c -> p t c", p=128)).then_inc(params_in, 16)
            sp.dma_start(b1_sb[:, :], b1.rearrange("(t p) -> p t", p=128),
                         allow_slow_non_contiguous=True).then_inc(params_in, 16)
            sp.dma_start(b2_sb[:, :], b2.rearrange("(c o) -> c o", o=1)).then_inc(params_in, 16)

            def batch(b, last):
                sp.wait_ge(y_stored, PRIMED_DMA + b * LOAD)
                load(xraw, b, xraw_in)
                if not last:
                    sp.wait_ge(ratio_ready, (b + 1) * PLANES_PB)
                    load(xn, b + 1, xn_in)
                for image in range(BATCH):
                    for g in range(GROUPS):
                        sp.wait_ge(y_ready, b * PLANES + plane_index(image, g) + 1)
                        store(image, g, lambda j: xraw[Q * j:Q * j + CG, image, g, :]
                              .rearrange("p (k w) -> p k w", w=W), y_q, b, y_stored)
                for image in range(BATCH):
                    for g in range(GROUPS):
                        sp.wait_ge(affine_done, b * LN_PLANES_PB + PLANES + plane_index(image, g) + 1)
                        store(image, g, lambda j: r_even[Q * j:Q * j + CG, image, g, :, 1:1 + W], n_q, b, n_stored)

            batches(sp, batch)

            sp.wait_ge(y_stored, PRIMED_DMA + N_BATCH * LOAD)
            sp.wait_ge(n_stored, PRIMED_DMA + N_BATCH * LOAD)
            n_t, y_t = mlp_tiles(n_dram), mlp_tiles(y_dram)

            def tiles(m, t, k):
                sp.wait_ge(hidden_done, PRIMED + 2 * k)
                for e in range(2):
                    sp.dma_start(m_n[:, e, :].rearrange("p (r w) -> p r w", w=W), n_t[m, e, t]).then_inc(mlp_n_in[e], 16)
                sp.wait_ge(out_ready, PRIMED + 2 * k)
                for e in range(2):
                    sp.dma_start(m_y[:, e, :].rearrange("p (r w) -> p r w", w=W), y_t[m, e, t]).then_inc(mlp_y_in[e], 16)

            mlp_loop(sp, tiles)
            sp.wait_ge(out_stored, PRIMED_DMA + 16 * 2 * MLP_PAIRS * MLP_TILES)

        @block.gpsimd
        def _(pool):
            pool.memset(xn[:, :, :, :], 0.0)
            pool.memset(xraw[:, :, :, :], 0.0).then_inc(buffers_cleared, 1)
            pool.memset(wt[:, :, :, :, :, :], 0.0)
            pool.memset(ln_par[:, :, :], 0.0).then_inc(buffers_cleared, 1)
            for n, eps in enumerate((EPS, LN1_EPS, LN2_EPS)):
                pool.memset(eps_sb[:, n:n + 1], eps)
            pool.memset(h_even[:, :, :, :, :], 0.0)
            pool.memset(h_odd[:, :, :, :, :], 0.0).then_inc(buffers_cleared, 1)

            def squares(b, src, ln, image):
                for g in range(GROUPS):
                    n = b * LN_PLANES_PB + ln * GROUPS + g
                    pool.wait_ge(centered, n + 1)
                    if g >= 2:
                        pool.wait_ge(square_summed, n - 1)
                    plane = src(image, g)
                    pool.tensor_tensor(flat(xseed[:, g % 2, :]), plane, plane, ALU.mult).then_inc(squared, 1)

            def xn_plane(image, g):
                return flat(xn[:, image, g, :])

            def group_sum(b, it, image):
                n = b * PLANES_PB + it * PLANES + image * GROUPS
                s = b * 2 * BATCH * N_ITER + it * 2 * BATCH + 2 * image
                total = flat(usum[:, image, :])
                pool.wait_ge(u_ready, PRIMED + n + 2)
                pool.tensor_tensor(total, inner(h_even, image, 0), inner(h_even, image, 1), ALU.add)\
                    .then_inc(part_done, 1)
                pool.wait_ge(u_ready, PRIMED + n + 4)
                pool.tensor_tensor(flat(upart[:, :]), inner(h_even, image, 2), inner(h_even, image, 3), ALU.add)\
                    .then_inc(part_done, 1)
                pool.wait_ge(part_done, s + 2)
                pool.tensor_tensor(usum[:, image, :], usum[:, image, :], upart[:, :], ALU.add)\
                    .then_inc(usum_ready, 1)

            def batch(b, last):
                for image in range(BATCH):
                    squares(b, xn_plane, image, image)

                with pool.Fori(0, N_ITER) as it:
                    pool.wait_ge(x_ready, (b + 1) * PLANES)
                    for p in range(PLANES):
                        image, g = divmod(p, GROUPS)
                        n = b * PLANES_PB + it * PLANES + p
                        pool.wait_ge(seed_ready, n + 1)
                        if p >= 2:
                            pool.wait_ge(ratio_ready, n - 1)
                        pool.tensor_tensor(xseed[:, p % 2, :], xn[:, image, g, :], seed[:, p % 2, :], ALU.mult)\
                            .then_inc(xseed_ready, 1)
                    for image in range(BATCH):
                        group_sum(b, it, image)

                for image in range(BATCH):
                    squares(b, lambda i, g: inner(r_even, i, g), BATCH + image, image)

            batches(pool, batch)

        @block.tensor
        def _(pe):
            for primed in (chan_done, hidden_done, mlp_done):
                pe.sem_inc(primed, PRIMED)
            pe.wait_ge(weights_ready, 1)
            pe.wait_ge(buffers_cleared, 3)
            pe.wait_ge(ones_set, 5)

            def unit_free(b, it, pos):
                if pos == 0:
                    return
                if pos == 2:
                    pe.wait_ge(x_ready, (b + 1) * PLANES)
                    return
                if pos == 1:
                    pe.wait_ge(u_ready, PRIMED + b * PLANES_PB + it * PLANES)
                    return
                what, image, g = ORDER[pos - PAIRS]
                if what == "T":
                    pe.wait_ge(prod_done, b * PLANES_PB + it * PLANES + (plane_index(image, g) + 1))
                elif what == "C":
                    pe.wait_ge(u_ready, PRIMED + b * PLANES_PB + it * PLANES + (plane_index(image, g) + 1))
                else:
                    pe.wait_ge(norm_step, b * STEPS_PB + it * (BATCH * INV_STEPS)
                               + (HEAD_STEPS + (1 - image) * INV_STEPS + 1))

            def ones_sum(slot, srcs, after_each=None, before_each=None):
                for n, src in enumerate(srcs):
                    if before_each:
                        before_each(n)
                    for half in range(2):
                        last = pe.matmul(ps[:, 2 * slot + half, 0:BANK].rearrange("p (s w) -> p s w", w=W),
                                         negones[:, :], src[:, half], start=n == 0, stop=n == len(srcs) - 1,
                                         skip_group_check=True)
                    if after_each:
                        last.then_inc(after_each, 1)
                return last

            def convolve(slot, kind, even, odd, image, g):
                for half in range(2):
                    for kx in range(3):
                        col = 2 - kx if kind == W_T else kx
                        for j in range(4):
                            src, first = [(odd, 0), (even, 0), (even, 0), (odd, 1)][j]
                            k0 = HALF * half + first
                            last = pe.matmul(
                                ps[Q * j:Q * (j + 1), 2 * slot + half, 0:BANK].rearrange("p (s w) -> p s w", w=W),
                                wt[:, kind, g, kx, 1 - j % 2, :],
                                src[:, image, g, k0:k0 + HALF, col:col + W],
                                start=kx == 0, stop=kx == 2, skip_group_check=True)
                return last

            def layer_norm(b, unit, ln, image, src):
                ones_sum(unit % PAIRS, [src(image, g) for g in range(GROUPS)]).then_inc(ln_sum_done, 1)
                n = b * LN_PLANES_PB + ln * GROUPS
                ones_sum((unit + 1) % PAIRS, [flat(xseed[:, g % 2, :]) for g in range(GROUPS)],
                         after_each=square_summed,
                         before_each=lambda g: pe.wait_ge(squared, n + g + 1))

            def batch(b, last):
                pe.wait_ge(scaled, PRIMED + b * LN_PLANES_PB)
                pe.wait_ge(xn_in, (b + 1) * LOAD)
                for image in range(BATCH):
                    unit = 3 * image
                    layer_norm(b, unit, image, image, lambda i, g: flat(xn[:, i, g, :]))
                    n = b * LN_PLANES_PB + image * GROUPS
                    ones_sum((unit + 2) % PAIRS, [flat(xn[:, image, g, :]) for g in range(GROUPS)],
                             before_each=lambda g: pe.wait_ge(affine_done, n + g + 1)).then_inc(ln_sum_done, 1)

                with pe.Fori(0, N_ITER) as it:
                    for pos, (what, image, g) in enumerate(ORDER):
                        unit_free(b, it, pos)
                        slot = (HEAD_UNITS + pos) % PAIRS
                        n = b * HB_PB + it * PLANES
                        if what == "T":
                            pe.wait_ge(h_both, PRIMED + n + (g + 1 if image == 0 else GROUPS + g + 1))
                            convolve(slot, W_T, h_even, h_odd, image, g).then_inc(recon_done, 1)
                        elif what == "C":
                            pe.wait_ge(ratio_both, b * PLANES_PB + it * PLANES + (plane_index(image, g) + 1))
                            convolve(slot, W_C, r_even, r_odd, image, g).then_inc(conv_done, 1)
                        else:
                            pe.wait_ge(usum_ready, b * US_PB + it * BATCH + (2 if image == 0 else 1))
                            ones_sum(slot, [flat(usum[:, image, :])]).then_inc(chan_done, 1)

                pe.wait_ge(norm_step, b * STEPS_PB + (HEAD_STEPS + N_ITER * BATCH * INV_STEPS))
                pe.wait_ge(usum_ready, (b + 1) * US_PB)
                ones_sum(TAIL % PAIRS, [flat(usum[:, 1, :])]).then_inc(chan_done, 1)
                for image in range(BATCH):
                    pe.wait_ge(y_ready, b * PLANES + (image + 1) * GROUPS)
                    layer_norm(b, TAIL + 1 + 2 * image, BATCH + image, image, lambda i, g: flat(xraw[:, i, g, :]))

            batches(pe, batch)

            pe.wait_ge(scaled, PRIMED + N_BATCH * LN_PLANES_PB)

            def tiles(m, t, k):
                for e in range(2):
                    pe.wait_ge(mlp_n_in[e], 16 * k + 16)
                    for c in range(HT):
                        last = pe.matmul(ps[:, HT * e + c, 0:MT], w1_sb[:, 128 * c:128 * (c + 1)], m_n[:, e, :],
                                         start=True, stop=True)
                    last.then_inc(hidden_done, 1)
                pe.wait_ge(out_ready, PRIMED + 2 * k)
                for e in range(2):
                    pe.wait_ge(gelu_done, 2 * k + (e + 1))
                    for c in range(HT):
                        last = pe.matmul(ps[0:C, 2 * HT + e, 0:MT], w2_sb[:, c, :], m_hid[:, HT * e + c, :],
                                         start=c == 0, stop=c == HT - 1)
                    last.then_inc(mlp_done, 1)

            mlp_loop(pe, tiles)

        @block.scalar
        def _(act):
            act.sem_inc(out_stored, PRIMED_DMA)
            act.preload_act_table_set("natural_log_exp_and_others")
            act.wait_ge(weight_step, WEIGHT_STEPS)
            act.wait_ge(buffers_cleared, 3)
            for kind, src, sign in ((W_T, w_nrm, -1.0), (W_C, w_tr, 1.0)):
                for ky in range(3):
                    dy = 1 - ky if kind == W_T else ky - 1
                    for variant in range(2):
                        q = 1 + variant + dy
                        for g in range(GROUPS):
                            last = act.activation(
                                wt[Q * q:Q * (q + 1), kind, g, :, variant, :],
                                src[Q * g:Q * (g + 1), 3 * Q * ky:3 * Q * (ky + 1)].rearrange("p (k m) -> p k m", m=Q),
                                ACT.Copy, scale=sign)
            last.then_inc(weights_ready, 1)
            act.wait_ge(params_in, 16 * N_PARAM_DMA)

            def log_exp(b_log, src, dst, eps, factor, power, signal):
                act.activation(dst, src, ACT.Ln, bias=eps_sb[:, eps:eps + 1], scale=factor).then_inc(log_done, 1)
                act.wait_ge(log_done, b_log + 1)
                act.activation(dst, dst, ACT.Exp, scale=power).then_inc(signal, 1)

            def norm_seed(b_log, unit):
                log_exp(b_log, pair(unit), flat(norm[:, 0, :]), 0, -1.0, -1.0, norm_seed_ready)

            def layer_norm(b, unit, ln, image, b_log, eps, buf, func, first_par):
                act.wait_ge(square_summed, b * LN_PLANES_PB + (ln + 1) * GROUPS)
                log_exp(b_log, pair(unit + 1), flat(norm[:, 0, :]), eps, -1.0 / C, -0.5, norm_seed_ready)
                for g in range(GROUPS):
                    act.wait_ge(scaled, PRIMED + b * LN_PLANES_PB + ln * GROUPS + g + 1)
                    plane = buf(image, g)
                    act.activation(plane, plane, func, scale=ln_par[:, first_par, g:g + 1],
                                   bias=ln_par[:, first_par + 1, g:g + 1]).then_inc(affine_done, 1)

            def copy_odd(even, odd, image, g):
                act.activation(odd[64:128, image, g, 0:SLOTS, 1:1 + W], even[0:64, image, g, :, 1:1 + W], ACT.Copy)
                return act.activation(odd[0:64, image, g, 1:SLOTS + 1, 1:1 + W],
                                      even[64:128, image, g, :, 1:1 + W], ACT.Copy)

            def batch(b, last):
                for image in range(BATCH):
                    layer_norm(b, 3 * image, image, image, b * LOGS_PB + 2 * image, 1,
                               lambda i, g: flat(xn[:, i, g, :]), ACT.Relu, 0)
                    act.wait_ge(ln_sum_done, b * SUMS_PB + 2 * image + 2)
                    norm_seed(b * LOGS_PB + 2 * image + 1, 3 * image + 2)

                with act.Fori(0, N_ITER) as it:
                    planes = b * PLANES_PB + it * PLANES
                    logs = b * LOGS_PB + it * LOGS_IT + HEAD_LOGS

                    def ratio_copy(image, g):
                        act.wait_ge(ratio_ready, planes + (plane_index(image, g) + 1))
                        copy_odd(r_even, r_odd, image, g).then_inc(ratio_both, 1)

                    n_log = 0
                    for pos, (what, image, g) in enumerate(ORDER):
                        unit = HEAD_UNITS + pos
                        if what == "T":
                            p = plane_index(image, g)
                            act.wait_ge(recon_done, planes + (p + 1))
                            if p >= 2:
                                act.wait_ge(ratio_ready, planes + (p - 1))
                            log_exp(logs + n_log, pair(unit), flat(seed[:, p % 2, :]), 0, -1.0, -1.0, seed_ready)
                            n_log += 1
                            if p >= 1:
                                ratio_copy(*divmod(p - 1, GROUPS))
                            if p == PLANES - 1:
                                ratio_copy(image, g)
                        elif what == "S":
                            act.wait_ge(chan_done, PRIMED + b * CH_PB + it * BATCH + (2 - image))
                            norm_seed(logs + n_log, unit)
                            n_log += 1

                logs = b * LOGS_PB + (HEAD_LOGS + N_ITER * LOGS_IT)
                act.wait_ge(chan_done, PRIMED + (b + 1) * CH_PB)
                norm_seed(logs, TAIL)
                for image in range(BATCH):
                    layer_norm(b, TAIL + 1 + 2 * image, BATCH + image, image, logs + (1 + image), 2,
                               lambda i, g: inner(r_even, i, g), ACT.Identity, 2)

            batches(act, batch)
            act.preload_act_table(ACT.Gelu)

            def tiles(m, t, k):
                act.wait_ge(mlp_done, PRIMED + 2 * k)
                for e in range(2):
                    act.wait_ge(hidden_done, PRIMED + 2 * k + (e + 1))
                    for c in range(HT):
                        last = act.activation(m_hid[:, HT * e + c, :], ps[:, HT * e + c, 0:MT], ACT.Gelu,
                                              bias=b1_sb[:, c:c + 1])
                    last.then_inc(gelu_done, 1)
                out_t = mlp_tiles(out)
                for e in range(2):
                    act.wait_ge(out_ready, PRIMED + 2 * k + (e + 1))
                    act.dma_start(out_t[m, e, t], m_out[:, e, :].rearrange("p (r w) -> p r w", w=W))\
                        .then_inc(out_stored, 16)

            mlp_loop(act, tiles)

        @block.vector
        def _(dve):
            for primed in (scaled, u_ready, h_both, out_ready):
                dve.sem_inc(primed, PRIMED)
            for n, buf in enumerate((seed, prod)):
                dve.memset(buf[:, :, :], 0.0).then_inc(w_cleared, 1) if n else dve.memset(buf[:, :, :], 0.0)
            dve.memset(negones[:, :], 0.0).then_inc(ones_set, 1)
            dve.wait_ge(ones_set, 1)
            for j in range(4):
                dve.memset(negones[Q * j:Q * j + CG, Q * j:Q * (j + 1)], -1.0).then_inc(ones_set, 1)
            dve.memset(r_even[:, :, :, :, :], 0.0)
            dve.memset(r_odd[:, :, :, :, :], 0.0)
            dve.wait_ge(buffers_cleared, 3)
            dve.wait_ge(w_in, 16 * GROUPS)
            dve.scalar_tensor_tensor(w_abs, w_raw, -1.0, w_raw, ALU.mult, ALU.max).then_inc(weight_step, 1)
            dve.wait_ge(weight_step, 1)
            dve.reduce_sum(w_sum, w_abs, AX.X).then_inc(weight_step, 1)
            dve.wait_ge(weight_step, 2)
            dve.tensor_scalar_add(w_sum, w_sum, EPS).then_inc(weight_step, 1)
            dve.wait_ge(weight_step, 3)
            dve.reciprocal(w_inv, w_sum).then_inc(weight_step, 1)
            dve.wait_ge(weight_step, 4)
            dve.tensor_scalar(w_nrm.rearrange("p (t i) -> p t i", i=Q)[:, :, 0:CG],
                              w_abs.rearrange("p (i t) -> p t i", i=CG), w_inv, None, ALU.mult).then_inc(weight_step, 1)
            dve.wait_ge(weight_step, 5)
            dve.transpose(w_tr, w_nrm).then_inc(weight_step, 1)

            def inverse(steps, unit):
                seed_n, prod_n, inv_n = (flat(norm[:, n, :]) for n in range(3))
                dve.scalar_tensor_tensor(prod_n, pair(unit), -EPS, seed_n, ALU.add, ALU.mult).then_inc(norm_step, 1)
                dve.wait_ge(norm_step, steps + 1)
                dve.scalar_tensor_tensor(inv_n, prod_n, 2.0, seed_n, ALU.add, ALU.mult).then_inc(norm_step, 1)
                dve.wait_ge(norm_step, steps + 2)

            def layer_norm(b, unit, ln, image, n_seed, sums, steps, eps, src, dst):
                dve.wait_ge(ln_sum_done, sums)
                for g in range(GROUPS):
                    last = dve.scalar_tensor_tensor(dst(image, g), pair(unit), 1.0 / C, src(image, g),
                                                    ALU.mult, ALU.add).then_inc(centered, 1)
                dve.wait_ge(centered, b * LN_PLANES_PB + (ln + 1) * GROUPS)
                y, v, s = (norm[:, n, :] for n in range(3))
                dve.wait_ge(norm_seed_ready, n_seed)
                dve.tensor_scalar(flat(v), pair(unit + 1), -1.0 / C, eps, ALU.mult, ALU.add).then_inc(norm_step, 1)
                dve.tensor_tensor(s, y, y, ALU.mult).then_inc(norm_step, 1)
                dve.wait_ge(norm_step, steps + 2)
                dve.tensor_tensor(v, v, s, ALU.mult).then_inc(norm_step, 1)
                dve.wait_ge(norm_step, steps + 3)
                dve.tensor_scalar(v, v, -0.5, 1.5, ALU.mult, ALU.add).then_inc(norm_step, 1)
                dve.wait_ge(norm_step, steps + 4)
                dve.tensor_tensor(s, v, y, ALU.mult).then_inc(norm_step, 1)
                dve.wait_ge(norm_step, steps + 5)
                for g in range(GROUPS):
                    plane = dst(image, g)
                    dve.tensor_tensor(plane, plane, flat(s), ALU.mult).then_inc(scaled, 1)

            def xn_plane(image, g):
                return flat(xn[:, image, g, :])

            def batch(b, last):
                dve.wait_ge(chan_done, PRIMED + b * CH_PB)
                for g in range(GROUPS):
                    dve.memset(h_odd[64:128, 0, g, 0:SLOTS, 1:1 + W], 1.0 / C)
                    dve.memset(h_odd[0:64, 0, g, 1:SLOTS + 1, 1:1 + W], 1.0 / C)
                    dve.memset(h_even[:, 0, g, :, 1:1 + W], 1.0 / C).then_inc(h_both, 1)
                for g in range(GROUPS):
                    dve.memset(h_even[:, 1, g, :, 1:1 + W], 1.0 / C)
                dve.memset(usum[:, 1, :], GROUPS / C).then_inc(usum_ready, 1)
                for image in range(BATCH):
                    steps = b * STEPS_PB + image * (LN_STEPS + INV_STEPS)
                    if image == 0:
                        dve.wait_ge(weights_ready, 1)
                        dve.wait_ge(xn_in, (b + 1) * LOAD)
                    layer_norm(b, 3 * image, image, image, b * NS_PB + (2 * image + 1),
                               b * SUMS_PB + (2 * image + 1), steps, LN1_EPS, xn_plane, xn_plane)
                    dve.wait_ge(norm_seed_ready, b * NS_PB + (2 * image + 2))
                    inverse(steps + LN_STEPS, 3 * image + 2)
                    dve.wait_ge(n_stored, PRIMED_DMA + b * LOAD)
                    for g in range(GROUPS):
                        plane = xn_plane(image, g)
                        dve.tensor_tensor(plane, plane, flat(norm[:, 2, :]), ALU.mult).then_inc(x_ready, 1)

                with dve.Fori(0, N_ITER) as it:
                    planes = b * PLANES_PB + it * PLANES

                    def normalise(image, g):
                        plane = inner(h_even, image, g)
                        dve.tensor_tensor(plane, plane, flat(norm[:, 2, :]), ALU.mult).then_inc(h_ready, 1)
                        dve.wait_ge(h_ready, b * H_PB + it * PLANES + ((1 - image) * GROUPS + g + 1))
                        dve.tensor_copy(h_odd[64:128, image, g, 0:SLOTS, 1:1 + W], h_even[0:64, image, g, :, 1:1 + W])
                        dve.tensor_copy(h_odd[0:64, image, g, 1:SLOTS + 1, 1:1 + W],
                                        h_even[64:128, image, g, :, 1:1 + W]).then_inc(h_both, 1)

                    def times_conv(image, g, unit):
                        dve.wait_ge(conv_done, planes + (plane_index(image, g) + 1))
                        plane = inner(h_even, image, g)
                        dve.tensor_tensor(plane, plane, pair(unit), ALU.mult).then_inc(u_ready, 1)

                    for pos, (what, image, g) in enumerate(ORDER):
                        unit = HEAD_UNITS + pos
                        if what == "T":
                            p = plane_index(image, g)
                            half_seed, half_prod, half_x = (flat(t[:, p % 2, :]) for t in (seed, prod, xseed))
                            dve.wait_ge(seed_ready, planes + (p + 1))
                            dve.scalar_tensor_tensor(half_prod, pair(unit), -EPS, half_seed, ALU.add, ALU.mult)\
                                .then_inc(prod_done, 1)
                            dve.wait_ge(prod_done, planes + (p + 1))
                            dve.wait_ge(xseed_ready, planes + (p + 1))
                            dve.scalar_tensor_tensor(inner(r_even, image, g), half_prod, 2.0, half_x,
                                                     ALU.add, ALU.mult).then_inc(ratio_ready, 1)
                            if p == 2:
                                normalise(1, 3)
                        elif what == "C":
                            times_conv(image, g, unit)
                        else:
                            dve.wait_ge(norm_seed_ready, b * NS_PB + it * BATCH + (HEAD_LOGS + 2 - image))
                            inverse(b * STEPS_PB + it * (BATCH * INV_STEPS)
                                    + (HEAD_STEPS + (1 - image) * INV_STEPS), unit)
                            for h in range(3):
                                normalise(image, h)
                            if image == 0:
                                normalise(image, 3)

                tail_steps = b * STEPS_PB + (HEAD_STEPS + N_ITER * BATCH * INV_STEPS)
                tail_seeds = b * NS_PB + (HEAD_LOGS + N_ITER * BATCH)
                dve.wait_ge(norm_seed_ready, tail_seeds + 1)
                inverse(tail_steps, TAIL)
                for g in range(GROUPS):
                    plane = inner(h_even, 1, g)
                    dve.tensor_tensor(plane, plane, flat(norm[:, 2, :]), ALU.mult).then_inc(h_ready, 1)
                dve.wait_ge(xraw_in, (b + 1) * LOAD)
                dve.wait_ge(h_ready, (b + 1) * H_PB)
                for image in range(BATCH):
                    for g in range(GROUPS):
                        plane = flat(xraw[:, image, g, :])
                        dve.tensor_tensor(plane, plane, inner(h_even, image, g), ALU.add).then_inc(y_ready, 1)
                for image in range(BATCH):
                    layer_norm(b, TAIL + 1 + 2 * image, BATCH + image, image, tail_seeds + (2 + image),
                               b * SUMS_PB + (HEAD_SUMS + image + 1), tail_steps + (INV_STEPS + image * LN_STEPS),
                               LN2_EPS, lambda i, g: flat(xraw[:, i, g, :]), lambda i, g: inner(r_even, i, g))

            batches(dve, batch)

            def tiles(m, t, k):
                dve.wait_ge(out_stored, PRIMED_DMA + 16 * 2 * k)
                for e in range(2):
                    dve.wait_ge(mlp_done, PRIMED + 2 * k + (e + 1))
                    dve.wait_ge(mlp_y_in[e], 16 * k + 16)
                    dve.scalar_tensor_tensor(m_out[:, e, :], ps[0:C, 2 * HT + e, 0:MT], b2_sb[:, 0:1], m_y[:, e, :],
                                             ALU.add, ALU.add).then_inc(out_ready, 1)

            mlp_loop(dve, tiles)


_INS = ["x", "L0_conv_ln1_w", "L0_conv_ln1_b", "L0_conv_w_nnmf", "L0_conv_ln2_w", "L0_conv_ln2_b",
        "L0_conv_w1", "L0_conv_b1", "L0_conv_w2", "L0_conv_b2"]


def kernel(**inputs):
    import numpy as _np
    import concourse.bacc as _bacc
    from concourse import mybir as _mybir
    from concourse.bass_utils import run_bass_kernel_spmd as _run

    nc = _bacc.Bacc("TRN2", target_bir_lowering=False, num_devices=1)
    arrays, args = {}, []
    for name in _INS:
        a = _np.ascontiguousarray(inputs[name])
        arrays[f"in_{name}_dram"] = a
        args.append(nc.dram_tensor(f"in_{name}_dram", a.shape, _mybir.dt.from_np(a.dtype), kind="ExternalInput").ap())
    args.append(nc.dram_tensor("out_dram", (N_IMG, C, H, W), _mybir.dt.float32, kind="ExternalOutput").ap())
    build_nnmf_block(nc, *args)
    r = _run(nc, [arrays], core_ids=[0])
    return r.results[0]["out_dram"]
```

```python
import numpy as np
import concourse.bass as bass
from concourse import mybir
from contextlib import ExitStack

N_IMG, C, H, W = 8, 96, 56, 56
GROUPS = 4
CG = C // GROUPS
HID = 384
N_ITER = 25
EPS = 1e-12
LN1_EPS = 1e-6
LN2_EPS = 1e-5
Q = 32
SLOTS = H // 4
WP = W + 2
R_SLOTS = SLOTS + 1
BANK = 512
PLANE, R_PLANE = SLOTS * W, R_SLOTS * W
SPLIT = 7
WP16 = W + 4
H_SCALE, W_SCALE = 2.0 ** 15, 2.0 ** 15
R_SCALE = H_SCALE * W_SCALE
BATCH = 2
N_BATCH = N_IMG // BATCH
PLANES = BATCH * GROUPS
PAIRS = 3
SPARE = -1

ORDER = [("C", 0, 0), ("C", 0, 1), ("T", 1, 0), ("C", 0, 2), ("T", 1, 1), ("C", 0, 3), ("T", 1, 2), ("S", 0, 0),
         ("T", 1, 3),
         ("C", 1, 0), ("C", 1, 1), ("T", 0, 0), ("C", 1, 2), ("T", 0, 1), ("C", 1, 3), ("T", 0, 2), ("S", 1, 0),
         ("T", 0, 3)]
LAST_ORDER = [step for step in ORDER if step[:2] != ("T", 0)]
ITER_UNITS = len(ORDER)
assert ITER_UNITS % PAIRS == 0
HEAD_UNITS = 3 * BATCH
FIRST_UNITS = GROUPS
assert HEAD_UNITS % PAIRS == 0


def plane_index(image, g):
    return image * GROUPS + g


def build_nnmf_block(nc, x, ln1_w, ln1_b, w_nnmf, ln2_w, ln2_b, w1, b1, w2, b2, out):
    f32 = mybir.dt.float32
    ALU = mybir.AluOpType
    ACT = mybir.ActivationFunctionType
    AX = mybir.AxisListType

    y_dram = nc.dram_tensor("y_scratch", (N_IMG, C, H, W), f32, kind="Internal").ap()
    n_dram = nc.dram_tensor("n_scratch", (N_IMG, C, H, W), f32, kind="Internal").ap()

    def row_quads(t):
        return t.rearrange("n (g c) (k j) w -> n g j c k w", g=GROUPS, j=4)

    f16 = mybir.dt.float16
    h_first = H_SCALE / C
    h_first_hi = float(np.float16(h_first))
    h_first_lo = float(np.float16(h_first - h_first_hi))

    x_q, y_q, n_q = row_quads(x), row_quads(y_dram), row_quads(n_dram)

    with ExitStack() as ctx:
        def sb(name, shape, dt=f32):
            return ctx.enter_context(nc.sbuf_tensor(name, shape, dt))

        def sem(name):
            return ctx.enter_context(nc.semaphore(name))

        xn = sb("xn", [128, BATCH, GROUPS, R_PLANE])
        x_res = sb("x_res", [128, 2, PLANE])
        h = sb("h", [128, BATCH, GROUPS, PLANE])
        h_even = sb("h_even", [128, BATCH, GROUPS, 2, R_SLOTS, WP16], f16)
        h_odd = sb("h_odd", [128, BATCH, GROUPS, 2, R_SLOTS, WP16], f16)
        r_even = sb("r_even", [128, BATCH, GROUPS, R_SLOTS, WP])
        r_odd = sb("r_odd", [128, BATCH, GROUPS, SLOTS, WP])
        seed = sb("seed", [128, 2, R_PLANE])
        xseed = sb("xseed", [128, 2, R_PLANE])
        usum = sb("usum", [128, BATCH, PLANE])
        norm = sb("norm", [128, BATCH, R_PLANE])
        wt_t = sb("wt_t", [128, 2, GROUPS, 3, 2, Q], f16)
        wt_c = sb("wt_c", [128, GROUPS, 3, 2, Q])
        negones = sb("negones", [128, 128])
        ln_par = sb("ln_par", [128, 4, GROUPS])
        w1_sb = sb("w1_sb", [C, HID])
        w2_sb = sb("w2_sb", [128, HID // 128, C])
        b1_sb = sb("b1_sb", [128, HID // 128])
        b2_sb = sb("b2_sb", [C, 1])
        GUARDS = (EPS * R_SCALE, EPS * H_SCALE, EPS, LN1_EPS, LN2_EPS)
        G_R, G_H, G_X, G_LN1, G_LN2 = range(5)
        guard = sb("guard", [128, len(GUARDS)])
        ps = ctx.enter_context(nc.psum_tensor("ps", [128, 8 * BANK], f32))

        w_raw = seed[:, 0, 0:CG * 9]
        w_abs = seed[:, 0, CG * 9:2 * CG * 9]
        w_nrm = seed[:, 1, 0:9 * Q]
        w_tr = seed[:, 1, 9 * Q:18 * Q]
        w_hi = xseed[:, 0, 0:9 * Q // 2].bitcast(f16)
        w_lo = xseed[:, 1, 0:9 * Q // 2].bitcast(f16)
        w_sum = norm[:, 0, 0:1]
        w_inv = norm[:, 1, 0:1]

        MT_ROWS = 8
        MT = MT_ROWS * W
        xn_flat = xn[:, :, :, :].rearrange("p a g c -> p (a g c)")
        HT = HID // 128

        def carve(start, parts, count):
            return xn_flat[0:parts, start:start + count * MT].rearrange("p (n c) -> p n c", n=count)

        m_n, m_y = carve(0, C, 2), carve(2 * MT, C, 2)
        m_hid, m_out = carve(4 * MT, 128, 2 * HT), carve((4 + 2 * HT) * MT, C, 2)

        def rows(ap):
            return ap.rearrange("p (s w) -> p s w", w=W)

        def unit_slots(unit, slots):
            pair = PAIRS if unit == SPARE else unit % PAIRS
            start = 2 * BANK * pair + BANK - W * (slots - SPLIT)
            return rows(ps[:, start:start + W * slots])

        def halves(slots):
            return (0, slots - SPLIT), (slots - SPLIT, slots)

        w_cleared = sem("w_cleared")
        ones_set = sem("ones_set")
        w_in = sem("w_in")
        params_in = sem("params_in")
        buffers_cleared = sem("buffers_cleared")
        weight_step = sem("weight_step")
        weights_ready = sem("weights_ready")
        xn_in = sem("xn_in")
        x_res_in = [sem("x_res_in0"), sem("x_res_in1"), sem("x_res_in2")]
        y_stored = sem("y_stored")
        n_stored = sem("n_stored")
        ln_sum_done = sem("ln_sum_done")
        centered = sem("centered")
        squared = sem("squared")
        square_summed = sem("square_summed")
        scaled = sem("scaled")
        affine_done = sem("affine_done")
        x_scaled = sem("x_scaled")
        x_ready = sem("x_ready")
        recon_done = sem("recon_done")
        conv_done = sem("conv_done")
        chan_done = sem("chan_done")
        log_done = sem("log_done")
        seed_ready = sem("seed_ready")
        norm_seed_ready = sem("norm_seed_ready")
        norm_step = sem("norm_step")
        xseed_ready = sem("xseed_ready")
        prod_done = sem("prod_done")
        hi_ready = sem("hi_ready")
        lo_ready = sem("lo_ready")
        h_set = sem("h_set")
        first_set = sem("first_set")
        ratio_ready = sem("ratio_ready")
        ratio_both = sem("ratio_both")
        u_ready = sem("u_ready")
        part_done = sem("part_done")
        usum_ready = sem("usum_ready")
        h_ready = sem("h_ready")
        h_both = sem("h_both")
        y_ready = sem("y_ready")
        mlp_n_in = [sem("mlp_n_in0"), sem("mlp_n_in1")]
        mlp_y_in = [sem("mlp_y_in0"), sem("mlp_y_in1")]
        hidden_done = sem("hidden_done")
        gelu_done = sem("gelu_done")
        mlp_done = sem("mlp_done")
        out_ready = sem("out_ready")
        out_stored = sem("out_stored")

        block = ctx.enter_context(nc.Block())

        PLANES_PB = N_ITER * PLANES
        HI_PB = PLANES_PB - GROUPS
        H_PB = PLANES_PB + GROUPS
        US_PB = N_ITER * BATCH
        LNS = 2 * BATCH
        LN_PLANES_PB = LNS * GROUPS
        HEAD_SUMS = 2 * BATCH
        SUMS_PB = HEAD_SUMS + BATCH
        HEAD_LOGS = 2 * BATCH
        LOGS_IT = PLANES + BATCH
        LOGS_PB = HEAD_LOGS + N_ITER * LOGS_IT + BATCH
        NS_PB = HEAD_LOGS + N_ITER * BATCH + BATCH
        LN_STEPS, INV_STEPS = 3, 2
        HEAD_STEPS = BATCH * (LN_STEPS + INV_STEPS)
        STEPS_PB = HEAD_STEPS + N_ITER * BATCH * INV_STEPS + BATCH * LN_STEPS
        WEIGHT_STEPS = 8
        N_PARAM_DMA = 4 * 4 + 4
        LOAD = 16 * 4 * PLANES
        PRIMED, PRIMED_DMA = 1, 16
        LOOP = HEAD_UNITS + FIRST_UNITS
        TAIL = LOOP + len(LAST_ORDER)

        HEAD_MEANS, TAIL_MEANS = (SPARE, 1), (TAIL, TAIL + 1)

        def residual_plane(n):
            if n < GROUPS:
                return r_odd[:, 0, n, :, 1:1 + W], 0
            if n < GROUPS + 2:
                return rows(x_res[:, n - GROUPS, :]), 1
            return r_odd[:, 1, n - GROUPS - 2, :, 1:1 + W], 2

        RESIDUAL_PLANES = (GROUPS, 2, 2)

        def t_rank(image, g):
            return plane_index(image, g) + (PLANES if image == 0 else 0)

        def iterations(eng, body):
            with eng.Fori(0, N_ITER - 1) as it:
                body(it, ORDER)
            body(N_ITER - 1, LAST_ORDER)

        def batches(eng, body):
            with eng.Fori(0, N_BATCH - 1) as b:
                body(b, False)
            body(N_BATCH - 1, True)

        MLP_PAIRS, MLP_TILES = N_IMG // 2, H // MT_ROWS

        def mlp_loop(eng, body):
            with eng.Fori(0, MLP_PAIRS) as m:
                with eng.Fori(0, MLP_TILES) as t:
                    body(m, t, m * MLP_TILES + t)

        def mlp_tiles(t):
            return t.rearrange("(m e) c (t r) w -> m e t c r w", e=2, r=MT_ROWS)

        @block.sync
        def _(sp):
            sp.sem_inc(y_stored, PRIMED_DMA)
            sp.sem_inc(n_stored, PRIMED_DMA)
            sp.wait_ge(w_cleared, 1)
            for g in range(GROUPS):
                sp.dma_start(w_raw[Q * g:Q * g + CG, :],
                             w_nnmf[CG * g:CG * (g + 1)].rearrange("o i a b -> o (i a b)")).then_inc(w_in, 16)

            def load_x(b):
                for image in range(BATCH):
                    for g in range(GROUPS):
                        for j in range(4):
                            q = (j + 1) % 4
                            first = 1 if q == 0 else 0
                            sp.dma_start(rows(xn[Q * q:Q * q + CG, image, g, :])[:, first:first + SLOTS, :],
                                         x_q[b * BATCH + image, g, j]).then_inc(xn_in, 16)

            def load_residual(b, n):
                image, g = divmod(n, GROUPS)
                place, group = residual_plane(n)
                for j in range(4):
                    sp.dma_start(place[Q * j:Q * j + CG], x_q[b * BATCH + image, g, j])\
                        .then_inc(x_res_in[group], 16)

            sp.wait_ge(buffers_cleared, 1)
            load_x(0)
            sp.wait_ge(buffers_cleared, 2)
            for n, par in enumerate((ln1_w, ln1_b, ln2_w, ln2_b)):
                for j in range(4):
                    sp.dma_start(ln_par[Q * j:Q * j + CG, n, :], par.rearrange("(g c) -> c g", c=CG),
                                 allow_slow_non_contiguous=True).then_inc(params_in, 16)
            sp.dma_start(w1_sb[:, :], w1[:, :]).then_inc(params_in, 16)
            sp.dma_start(w2_sb[:, :, :], w2.rearrange("(t p) c -> p t c", p=128)).then_inc(params_in, 16)
            sp.dma_start(b1_sb[:, :], b1.rearrange("(t p) -> p t", p=128),
                         allow_slow_non_contiguous=True).then_inc(params_in, 16)
            sp.dma_start(b2_sb[:, :], b2.rearrange("(c o) -> c o", o=1)).then_inc(params_in, 16)

            def batch(b, last):
                load_residual(b, GROUPS)
                load_residual(b, GROUPS + 1)
                for n in range(GROUPS):
                    sp.wait_ge(conv_done, b * PLANES_PB + ((N_ITER - 1) * PLANES + n + 1))
                    load_residual(b, n)
                for n in range(2):
                    sp.wait_ge(conv_done, b * PLANES_PB + ((N_ITER - 1) * PLANES + GROUPS + n + 1))
                    load_residual(b, GROUPS + 2 + n)
                if not last:
                    sp.wait_ge(ratio_ready, (b + 1) * PLANES_PB)
                    load_x(b + 1)
                for n in range(PLANES):
                    image, g = divmod(n, GROUPS)
                    sp.wait_ge(y_ready, b * PLANES + n + 1)
                    for j in range(4):
                        sp.dma_start(y_q[b * BATCH + image, g, j], rows(h[Q * j:Q * j + CG, image, g, :]))\
                            .then_inc(y_stored, 16)
                for n in range(PLANES):
                    image, g = divmod(n, GROUPS)
                    sp.wait_ge(affine_done, b * LN_PLANES_PB + PLANES + n + 1)
                    for j in range(4):
                        sp.dma_start(n_q[b * BATCH + image, g, j],
                                     r_even[Q * j:Q * j + CG, image, g, 0:SLOTS, 1:1 + W]).then_inc(n_stored, 16)

            batches(sp, batch)

            sp.wait_ge(y_stored, PRIMED_DMA + N_BATCH * LOAD)
            sp.wait_ge(n_stored, PRIMED_DMA + N_BATCH * LOAD)
            n_t, y_t = mlp_tiles(n_dram), mlp_tiles(y_dram)

            def tiles(m, t, k):
                sp.wait_ge(hidden_done, PRIMED + 2 * k)
                for e in range(2):
                    sp.dma_start(m_n[:, e, :].rearrange("p (r w) -> p r w", w=W), n_t[m, e, t]).then_inc(mlp_n_in[e], 16)
                sp.wait_ge(out_ready, PRIMED + 2 * k)
                for e in range(2):
                    sp.dma_start(m_y[:, e, :].rearrange("p (r w) -> p r w", w=W), y_t[m, e, t]).then_inc(mlp_y_in[e], 16)

            mlp_loop(sp, tiles)
            sp.wait_ge(out_stored, PRIMED_DMA + 16 * 2 * MLP_PAIRS * MLP_TILES)

        @block.gpsimd
        def _(pool):
            pool.memset(xn[:, :, :, :], 0.0)
            pool.memset(x_res[:, :, :], 0.0).then_inc(buffers_cleared, 1)
            pool.memset(wt_t[:, :, :, :, :, :], 0.0)
            pool.memset(wt_c[:, :, :, :, :], 0.0)
            pool.memset(ln_par[:, :, :], 0.0).then_inc(buffers_cleared, 1)
            for n, eps in enumerate(GUARDS):
                pool.memset(guard[:, n:n + 1], eps)
            pool.memset(h_even[:, :, :, :, :, :].bitcast(f32), 0.0)
            pool.memset(h_odd[:, :, :, :, :, :].bitcast(f32), 0.0).then_inc(buffers_cleared, 1)

            def first_h():
                pool.memset(h_even[:, 0, :, 0, 0:SLOTS, 2:2 + W], h_first_hi)
                pool.memset(h_even[:, 0, :, 1, 0:SLOTS, 2:2 + W], h_first_lo)
                pool.memset(h_odd[:, 0, :, 0, 1:SLOTS, 2:2 + W], h_first_hi)
                pool.memset(h_odd[:, 0, :, 1, 1:SLOTS, 2:2 + W], h_first_lo).then_inc(h_set, 1)

            pool.wait_ge(buffers_cleared, 3)
            first_h()

            def xseed_plane(rank, image, g, first=False):
                pool.wait_ge(seed_ready, rank + 1)
                if not first:
                    pool.wait_ge(ratio_ready, rank - 1)
                pool.tensor_tensor(xseed[:, g % 2, :], xn[:, image, g, :], seed[:, g % 2, :], ALU.mult)\
                    .then_inc(xseed_ready, 1)

            def batch(b, last):
                pool.wait_ge(x_ready, (b + 1) * PLANES)
                for g in range(GROUPS):
                    xseed_plane(b * PLANES_PB + g, 0, g, g < 2)

                def iteration(it, order):
                    planes = b * PLANES_PB + it * PLANES
                    for what, image, g in order:
                        if what == "T":
                            xseed_plane(planes + t_rank(image, g), image, g)
                        elif what == "C" and g == 1:
                            pool.wait_ge(u_ready, planes + (plane_index(image, g) + 1))
                            pool.tensor_tensor(usum[:, image, :], h[:, image, 0, :], h[:, image, 1, :], ALU.add)\
                                .then_inc(part_done, 1)
                        elif what == "C" and g == 2:
                            parts = b * 2 * US_PB + it * (2 * BATCH) + 2 * image
                            pool.wait_ge(u_ready, planes + (plane_index(image, g) + 1))
                            pool.wait_ge(part_done, parts + 1)
                            pool.tensor_tensor(usum[:, image, :], usum[:, image, :], h[:, image, 2, :], ALU.add)\
                                .then_inc(part_done, 1)

                iterations(pool, iteration)
                if not last:
                    first_h()

            batches(pool, batch)

        @block.tensor
        def _(pe):
            for primed in (hidden_done, mlp_done):
                pe.sem_inc(primed, PRIMED)
            pe.wait_ge(weights_ready, 1)
            pe.wait_ge(buffers_cleared, 3)
            pe.wait_ge(ones_set, 5)

            def unit_free(b, it, order, pos):
                planes = b * PLANES_PB + it * PLANES
                earlier = 0 if pos >= PAIRS else 1
                what, image, g = order[pos - PAIRS] if pos >= PAIRS else ORDER[pos - PAIRS]
                if what == "T":
                    pe.wait_ge(ratio_ready, planes + (t_rank(image, g) + 1 - earlier * PLANES))
                elif what == "C":
                    pe.wait_ge(u_ready, planes + (plane_index(image, g) + 1))
                else:
                    pe.wait_ge(norm_step, b * STEPS_PB + it * (BATCH * INV_STEPS)
                               + (HEAD_STEPS + (image + 1 - earlier * BATCH) * INV_STEPS))

            def bank_part(unit, slots, half):
                a, e = halves(slots)[half]
                return unit_slots(unit, slots)[:, a:e, :], a, e

            def ones_sum(unit, slots, srcs, after_each=None, before_each=None):
                for n, src in enumerate(srcs):
                    if before_each:
                        before_each(n)
                    for half in range(2):
                        dst, a, e = bank_part(unit, slots, half)
                        last = pe.matmul(dst, negones[:, :], src[:, a:e, :], start=n == 0, stop=n == len(srcs) - 1,
                                         skip_group_check=True)
                    if after_each:
                        last.then_inc(after_each, 1)
                return last

            def transposed_conv(unit, image, g):
                for half in range(2):
                    dst, a, e = bank_part(unit, R_SLOTS, half)
                    for kx in range(3):
                        col = 1 + 2 - kx
                        for part, (w_part, h_part) in enumerate(((0, 0), (1, 0), (0, 1))):
                            for tile, src in ((0, h_odd), (64, h_even)):
                                last = pe.matmul(dst[tile:tile + 64], wt_t[:, w_part, g, kx, :, :]
                                                 .rearrange("p a b -> p (a b)"),
                                                 src[:, image, g, h_part, a:e, col:col + W],
                                                 start=kx == 0 and part == 0, stop=kx == 2 and part == 2,
                                                 skip_group_check=True)
                return last

            def conv(unit, image, g):
                for half in range(2):
                    dst, a, e = bank_part(unit, SLOTS, half)
                    for kx in range(3):
                        for tile, src in ((0, r_even), (64, r_odd)):
                            last = pe.matmul(dst[tile:tile + 64], wt_c[:, g, kx, :, :].rearrange("p a b -> p (a b)"),
                                             src[:, image, g, a:e, kx:kx + W],
                                             start=kx == 0, stop=kx == 2, skip_group_check=True)
                return last

            def means(units, slots, src, before):
                for image in range(BATCH):
                    before(image)
                    ones_sum(units[image], slots, [src(image, g) for g in range(GROUPS)]).then_inc(ln_sum_done, 1)

            def variances(b, first, slots, ln):
                for image in range(BATCH):
                    n = b * LN_PLANES_PB + (ln + image) * GROUPS
                    ones_sum(first + image, slots, [rows(xseed[:, g % 2, 0:slots * W]) for g in range(GROUPS)],
                             after_each=square_summed, before_each=lambda g: pe.wait_ge(squared, n + g + 1))

            def batch(b, last):
                pe.wait_ge(xn_in, (b + 1) * LOAD)
                means(HEAD_MEANS, R_SLOTS, lambda i, g: rows(xn[:, i, g, :]), lambda i: None)
                variances(b, BATCH, R_SLOTS, 0)
                for image in range(BATCH):
                    n = b * LN_PLANES_PB + image * GROUPS
                    ones_sum(2 * BATCH + image, R_SLOTS, [rows(xn[:, image, g, :]) for g in range(GROUPS)],
                             before_each=lambda g: pe.wait_ge(affine_done, n + g + 1)).then_inc(ln_sum_done, 1)

                for g in range(GROUPS):
                    if g in (1, 2):
                        pe.wait_ge(norm_step, b * STEPS_PB + (HEAD_STEPS - (2 - g) * INV_STEPS))
                    elif g == 3:
                        pe.wait_ge(ratio_ready, b * PLANES_PB + 1)
                    pe.wait_ge(h_both, b * PLANES_PB + (g + 1))
                    transposed_conv(HEAD_UNITS + g, 0, g).then_inc(recon_done, 1)

                def iteration(it, order):
                    planes = b * PLANES_PB + it * PLANES
                    for pos, (what, image, g) in enumerate(order):
                        unit_free(b, it, order, pos)
                        unit = LOOP + pos
                        if what == "T":
                            pe.wait_ge(h_both, planes + (t_rank(image, g) + 1))
                            transposed_conv(unit, image, g).then_inc(recon_done, 1)
                        elif what == "C":
                            pe.wait_ge(ratio_both, planes + (plane_index(image, g) + 1))
                            conv(unit, image, g).then_inc(conv_done, 1)
                        else:
                            pe.wait_ge(usum_ready, b * US_PB + it * BATCH + (image + 1))
                            ones_sum(unit, SLOTS, [rows(usum[:, image, :])]).then_inc(chan_done, 1)

                iterations(pe, iteration)

                pe.wait_ge(u_ready, (b + 1) * PLANES_PB)
                means(TAIL_MEANS, SLOTS, lambda i, g: rows(h[:, i, g, :]),
                      lambda i: pe.wait_ge(y_ready, b * PLANES + (i + 1) * GROUPS))
                variances(b, TAIL + BATCH, SLOTS, BATCH)

            batches(pe, batch)

            pe.wait_ge(scaled, PRIMED + N_BATCH * LN_PLANES_PB)

            def tiles(m, t, k):
                for e in range(2):
                    pe.wait_ge(mlp_n_in[e], 16 * k + 16)
                    for c in range(HT):
                        last = pe.matmul(ps[:, BANK * (HT * e + c):BANK * (HT * e + c) + MT], w1_sb[:, 128 * c:128 * (c + 1)], m_n[:, e, :],
                                         start=True, stop=True)
                    last.then_inc(hidden_done, 1)
                pe.wait_ge(out_ready, PRIMED + 2 * k)
                for e in range(2):
                    pe.wait_ge(gelu_done, 2 * k + (e + 1))
                    for c in range(HT):
                        last = pe.matmul(ps[0:C, BANK * (2 * HT + e):BANK * (2 * HT + e) + MT], w2_sb[:, c, :], m_hid[:, HT * e + c, :],
                                         start=c == 0, stop=c == HT - 1)
                    last.then_inc(mlp_done, 1)

            mlp_loop(pe, tiles)

        @block.scalar
        def _(act):
            act.sem_inc(out_stored, PRIMED_DMA)
            act.preload_act_table_set("natural_log_exp_and_others")
            act.wait_ge(weight_step, WEIGHT_STEPS)
            act.wait_ge(buffers_cleared, 3)
            for ky in range(3):
                for row in range(2):
                    for g in range(GROUPS):
                        def spread(dst, src, q):
                            return act.activation(
                                dst[Q * q:Q * (q + 1), g, :, row, :],
                                src[Q * g:Q * (g + 1), 3 * Q * ky:3 * Q * (ky + 1)]
                                .rearrange("p (k m) -> p k m", m=Q), ACT.Copy)
                        spread(wt_t[:, 0], w_hi, 1 + row + 1 - ky)
                        spread(wt_t[:, 1], w_lo, 1 + row + 1 - ky)
                        last = spread(wt_c, w_tr, 1 + row + ky - 1)
            last.then_inc(weights_ready, 1)
            act.wait_ge(params_in, 16 * N_PARAM_DMA)

            def log_exp(log_count, src, dst, eps, factor, power, signal):
                act.activation(dst, src, ACT.Ln, bias=guard[:, eps:eps + 1], scale=factor).then_inc(log_done, 1)
                act.wait_ge(log_done, log_count + 1)
                act.activation(dst, dst, ACT.Exp, scale=power).then_inc(signal, 1)

            def norm_seed(log_count, unit, slots, image, eps):
                log_exp(log_count, unit_slots(unit, slots), rows(norm[:, image, 0:slots * W]), eps, -1.0, -1.0,
                        norm_seed_ready)

            def layer_norms(b, first_var, slots, ln, log_count, eps, plane, func, first_par):
                for image in range(BATCH):
                    for g in range(GROUPS):
                        n = b * LN_PLANES_PB + (ln + image) * GROUPS + g
                        act.wait_ge(centered, n + 1)
                        if image or g >= 2:
                            act.wait_ge(square_summed, n - 1)
                        act.activation(rows(xseed[:, g % 2, 0:slots * W]), plane(image, g), ACT.Square)\
                            .then_inc(squared, 1)
                for image in range(BATCH):
                    act.wait_ge(square_summed, b * LN_PLANES_PB + (ln + image + 1) * GROUPS)
                    log_exp(log_count + image, unit_slots(first_var + image, slots),
                            rows(norm[:, image, 0:slots * W]), eps, -1.0 / C, -0.5, norm_seed_ready)
                for image in range(BATCH):
                    for g in range(GROUPS):
                        act.wait_ge(scaled, PRIMED + b * LN_PLANES_PB + (ln + image) * GROUPS + g + 1)
                        act.activation(plane(image, g), plane(image, g), func, scale=ln_par[:, first_par, g:g + 1],
                                       bias=ln_par[:, first_par + 1, g:g + 1]).then_inc(affine_done, 1)

            def batch(b, last):
                act.wait_ge(h_set, b + 1)
                act.activation(h_odd[64:128, 0, :, :, 0, 2:2 + W], h_even[0:64, 0, :, :, 0, 2:2 + W], ACT.Copy)
                act.activation(h_odd[0:64, 0, :, :, SLOTS, 2:2 + W], h_even[64:128, 0, :, :, SLOTS - 1, 2:2 + W],
                               ACT.Copy).then_inc(h_both, GROUPS)
                layer_norms(b, BATCH, R_SLOTS, 0, b * LOGS_PB, G_LN1, lambda i, g: rows(xn[:, i, g, :]), ACT.Relu, 0)
                for image in range(BATCH):
                    act.wait_ge(ln_sum_done, b * SUMS_PB + BATCH + image + 1)
                    norm_seed(b * LOGS_PB + BATCH + image, 2 * BATCH + image, R_SLOTS, image, G_X)

                def seed_plane(log_count, rank, unit, g, first=False):
                    act.wait_ge(recon_done, rank + 1)
                    if not first:
                        act.wait_ge(ratio_ready, rank - 1)
                    log_exp(log_count, unit_slots(unit, R_SLOTS), rows(seed[:, g % 2, :]), G_R, -1.0, -1.0,
                            seed_ready)

                def ratio_copy(rank, image, g):
                    act.wait_ge(ratio_ready, rank + 1)
                    act.activation(r_odd[0:64, image, g, :, 1:1 + W], r_even[64:128, image, g, 0:SLOTS, 1:1 + W],
                                   ACT.Copy)
                    act.activation(r_odd[64:128, image, g, :, 1:1 + W],
                                   r_even[0:64, image, g, 1:R_SLOTS, 1:1 + W], ACT.Copy).then_inc(ratio_both, 1)

                for g in range(GROUPS):
                    rank = b * PLANES_PB + g
                    seed_plane(b * LOGS_PB + (HEAD_LOGS + g), rank, HEAD_UNITS + g, g, g < 2)
                    if g:
                        ratio_copy(rank - 1, 0, g - 1)

                def iteration(it, order):
                    planes = b * PLANES_PB + it * PLANES
                    logs = b * LOGS_PB + it * LOGS_IT + (HEAD_LOGS + GROUPS)
                    n_log = 0
                    for pos, (what, image, g) in enumerate(order):
                        if what == "T":
                            rank = t_rank(image, g)
                            seed_plane(logs + n_log, planes + rank, LOOP + pos, g)
                            ratio_copy(planes + (rank - 1), *divmod((rank - 1) % PLANES, GROUPS))
                            n_log += 1
                        elif what == "S":
                            act.wait_ge(chan_done, b * US_PB + it * BATCH + (image + 1))
                            norm_seed(logs + n_log, LOOP + pos, SLOTS, image, G_H)
                            n_log += 1
                        if order is LAST_ORDER and (what, image, g) == ("T", 1, GROUPS - 1):
                            ratio_copy(planes + rank, image, g)

                iterations(act, iteration)

                layer_norms(b, TAIL + BATCH, SLOTS, BATCH, (b + 1) * LOGS_PB - BATCH, G_LN2,
                            lambda i, g: r_even[:, i, g, 0:SLOTS, 1:1 + W], ACT.Identity, 2)

            batches(act, batch)
            act.preload_act_table(ACT.Gelu)

            def tiles(m, t, k):
                act.wait_ge(mlp_done, PRIMED + 2 * k)
                for e in range(2):
                    act.wait_ge(hidden_done, PRIMED + 2 * k + (e + 1))
                    for c in range(HT):
                        last = act.activation(m_hid[:, HT * e + c, :], ps[:, BANK * (HT * e + c):BANK * (HT * e + c) + MT], ACT.Gelu,
                                              bias=b1_sb[:, c:c + 1])
                    last.then_inc(gelu_done, 1)
                out_t = mlp_tiles(out)
                for e in range(2):
                    act.wait_ge(out_ready, PRIMED + 2 * k + (e + 1))
                    act.dma_start(out_t[m, e, t], m_out[:, e, :].rearrange("p (r w) -> p r w", w=W))\
                        .then_inc(out_stored, 16)

            mlp_loop(act, tiles)

        @block.vector
        def _(dve):
            for primed in (scaled, out_ready):
                dve.sem_inc(primed, PRIMED)
            dve.memset(seed[:, :, :], 0.0).then_inc(w_cleared, 1)
            dve.memset(negones[:, :], 0.0).then_inc(ones_set, 1)
            dve.wait_ge(ones_set, 1)
            for j in range(4):
                dve.memset(negones[Q * j:Q * j + CG, Q * j:Q * (j + 1)], -1.0).then_inc(ones_set, 1)
            dve.memset(r_even[:, :, :, :, :], 0.0)
            dve.memset(r_odd[:, :, :, :, :], 0.0)
            dve.wait_ge(buffers_cleared, 3)
            dve.wait_ge(w_in, 16 * GROUPS)
            dve.scalar_tensor_tensor(w_abs, w_raw, -1.0, w_raw, ALU.mult, ALU.max).then_inc(weight_step, 1)
            dve.wait_ge(weight_step, 1)
            dve.reduce_sum(w_sum, w_abs, AX.X).then_inc(weight_step, 1)
            dve.wait_ge(weight_step, 2)
            dve.tensor_scalar_add(w_sum, w_sum, EPS).then_inc(weight_step, 1)
            dve.wait_ge(weight_step, 3)
            dve.reciprocal(w_inv, w_sum).then_inc(weight_step, 1)
            dve.wait_ge(weight_step, 4)
            dve.tensor_scalar(w_nrm.rearrange("p (t i) -> p t i", i=Q)[:, :, 0:CG],
                              w_abs.rearrange("p (i t) -> p t i", i=CG), w_inv, None, ALU.mult).then_inc(weight_step, 1)
            dve.wait_ge(weight_step, 5)
            dve.transpose(w_tr, w_nrm).then_inc(weight_step, 1)
            dve.tensor_scalar(w_hi, w_nrm, -W_SCALE, None, ALU.mult).then_inc(weight_step, 1)
            dve.wait_ge(weight_step, 7)
            dve.scalar_tensor_tensor(w_lo, w_nrm, -W_SCALE, w_hi, ALU.mult, ALU.subtract).then_inc(weight_step, 1)

            def inverse(steps, unit, slots, image, guard_value):
                prod, seed_n = unit_slots(unit, slots), rows(norm[:, image, 0:slots * W])
                dve.scalar_tensor_tensor(prod, prod, -guard_value, seed_n, ALU.add, ALU.mult).then_inc(norm_step, 1)
                dve.wait_ge(norm_step, steps + 1)
                dve.scalar_tensor_tensor(seed_n, prod, 2.0, seed_n, ALU.add, ALU.mult).then_inc(norm_step, 1)
                dve.wait_ge(norm_step, steps + 2)

            def centre(mean_units, slots, sums, src, dst):
                for image in range(BATCH):
                    dve.wait_ge(ln_sum_done, sums + image + 1)
                    for g in range(GROUPS):
                        dve.scalar_tensor_tensor(dst(image, g), unit_slots(mean_units[image], slots), 1.0 / C,
                                                 src(image, g), ALU.mult, ALU.add).then_inc(centered, 1)

            def scale_to_unit(first_var, slots, seeds, steps, eps, dst):
                for image in range(BATCH):
                    y, s = (rows(t[:, image, 0:slots * W]) for t in (norm, seed))
                    dve.wait_ge(norm_seed_ready, seeds + image + 1)
                    dve.tensor_tensor(s, y, y, ALU.mult).then_inc(norm_step, 1)
                    dve.wait_ge(norm_step, steps + image * LN_STEPS + 1)
                    dve.scalar_tensor_tensor(s, unit_slots(first_var + image, slots), -C * eps, s,
                                             ALU.add, ALU.mult).then_inc(norm_step, 1)
                    dve.wait_ge(norm_step, steps + image * LN_STEPS + 2)
                    dve.scalar_tensor_tensor(y, s, 3.0 * C, y, ALU.add, ALU.mult).then_inc(norm_step, 1)
                    dve.wait_ge(norm_step, steps + image * LN_STEPS + 3)
                    for g in range(GROUPS):
                        dve.scalar_tensor_tensor(dst(image, g), dst(image, g), 0.5 / C, y,
                                                 ALU.mult, ALU.mult).then_inc(scaled, 1)

            def xn_plane(image, g):
                return rows(xn[:, image, g, :])

            def normalise(image, g):
                dve.scalar_tensor_tensor(h[:, image, g, :], h[:, image, g, :], H_SCALE, norm[:, image, 0:PLANE],
                                         ALU.mult, ALU.mult).then_inc(h_ready, 1)

            def batch(b, last):
                dve.wait_ge(weights_ready, 1)
                dve.wait_ge(xn_in, (b + 1) * LOAD)
                centre(HEAD_MEANS, R_SLOTS, b * SUMS_PB, xn_plane, xn_plane)
                dve.wait_ge(y_stored, PRIMED_DMA + b * LOAD)
                dve.memset(h[:, 0, :, :], h_first)
                dve.memset(h[:, 1, :, :], 1.0)
                scale_to_unit(BATCH, R_SLOTS, b * NS_PB, b * STEPS_PB, LN1_EPS, xn_plane)
                for image in range(BATCH):
                    dve.wait_ge(norm_seed_ready, b * NS_PB + (BATCH + image + 1))
                    inverse(b * STEPS_PB + (BATCH * LN_STEPS + image * INV_STEPS), 2 * BATCH + image, R_SLOTS, image,
                            EPS)
                    dve.wait_ge(n_stored, PRIMED_DMA + b * LOAD)
                    for g in range(GROUPS):
                        dve.scalar_tensor_tensor(xn[:, image, g, :], xn[:, image, g, :], R_SCALE, norm[:, image, :],
                                                 ALU.mult, ALU.mult).then_inc(x_scaled, 1)
                    dve.wait_ge(x_scaled, b * PLANES + (image + 1) * GROUPS)
                    dve.memset(xn[0:Q, image, :, 0:W], 0.0)
                    dve.memset(xn[Q:2 * Q, image, :, PLANE:R_PLANE], 0.0)
                    dve.memset(xn[2 * Q:4 * Q, image, :, PLANE:R_PLANE], 0.0).then_inc(x_ready, GROUPS)

                dve.memset(norm[:, 1, 0:PLANE], 1.0 / C).then_inc(first_set, 1)
                dve.wait_ge(first_set, b + 1)

                def newton(rank, unit, g):
                    prod = unit_slots(unit, R_SLOTS)
                    dve.wait_ge(seed_ready, rank + 1)
                    dve.scalar_tensor_tensor(prod, prod, -EPS * R_SCALE, rows(seed[:, g % 2, :]),
                                             ALU.add, ALU.mult).then_inc(prod_done, 1)

                def ratio(rank, unit, image, g):
                    dve.wait_ge(prod_done, rank + 1)
                    dve.wait_ge(xseed_ready, rank + 1)
                    dve.scalar_tensor_tensor(r_even[:, image, g, :, 1:1 + W], unit_slots(unit, R_SLOTS), 2.0,
                                             rows(xseed[:, g % 2, :]), ALU.add, ALU.mult).then_inc(ratio_ready, 1)

                for g in range(GROUPS - 1):
                    newton(b * PLANES_PB + g, HEAD_UNITS + g, g)
                    ratio(b * PLANES_PB + g, HEAD_UNITS + g, 0, g)

                def residual(n):
                    image, g = divmod(n, GROUPS)
                    dve.wait_ge(h_ready, b * H_PB + (N_ITER * PLANES - GROUPS + n + 1))
                    place, group = residual_plane(n)
                    dve.wait_ge(x_res_in[group], (b + 1) * (16 * 4 * RESIDUAL_PLANES[group]))
                    dve.scalar_tensor_tensor(rows(h[:, image, g, :]), rows(h[:, image, g, :]), 1.0 / H_SCALE, place,
                                             ALU.mult, ALU.add).then_inc(y_ready, 1)

                def iteration(it, order):
                    planes = b * PLANES_PB + it * PLANES
                    last_iteration = order is LAST_ORDER

                    def split(image, g):
                        n = b * HI_PB + it * PLANES + ((1 - image) * GROUPS + g + 1)
                        high, low = (h_even[:, image, g, part, 0:SLOTS, 2:2 + W] for part in range(2))
                        dve.wait_ge(h_ready, b * H_PB + it * PLANES + ((1 - image) * GROUPS + g + 1))
                        dve.tensor_copy(high, rows(h[:, image, g, :])).then_inc(hi_ready, 1)
                        dve.wait_ge(hi_ready, n)
                        dve.tensor_tensor(low, rows(h[:, image, g, :]), high, ALU.subtract).then_inc(lo_ready, 1)
                        dve.wait_ge(lo_ready, n)
                        dve.tensor_copy(h_odd[64:128, image, g, :, 0:SLOTS, 2:2 + W],
                                        h_even[0:64, image, g, :, 0:SLOTS, 2:2 + W])
                        dve.tensor_copy(h_odd[0:64, image, g, :, 1:SLOTS + 1, 2:2 + W],
                                        h_even[64:128, image, g, :, 0:SLOTS, 2:2 + W]).then_inc(h_both, 1)

                    def product(image, g):
                        dve.wait_ge(conv_done, planes + (plane_index(image, g) + 1))
                        dve.tensor_tensor(rows(h[:, image, g, :]), rows(h[:, image, g, :]),
                                          unit_slots(LOOP + order.index(("C", image, g)), SLOTS), ALU.mult)\
                            .then_inc(u_ready, 1)

                    for ahead in range(BATCH):
                        behind = 1 - ahead
                        splits = not (last_iteration and behind == 0)

                        def t_args(image, g):
                            unit = LOOP + order.index(("T", image, g))
                            return planes + t_rank(image, g), unit

                        normalise(behind, 0)
                        if splits:
                            split(behind, 0)
                        rank = planes + plane_index(ahead, GROUPS - 1)
                        unit = LOOP + (ORDER.index(("T", ahead, GROUPS - 1)) if ahead else -1)
                        newton(rank, unit, GROUPS - 1)
                        ratio(rank, unit, ahead, GROUPS - 1)
                        product(ahead, 0)
                        normalise(behind, 1)
                        if splits:
                            split(behind, 1)
                        product(ahead, 1)
                        normalise(behind, 2)
                        if splits:
                            split(behind, 2)
                            newton(*t_args(behind, 0), 0)
                        normalise(behind, 3)
                        if splits:
                            rank, unit = t_args(behind, 0)
                            ratio(rank, unit, behind, 0)
                        product(ahead, 2)
                        if splits:
                            split(behind, 3)
                            rank, unit = t_args(behind, 1)
                            newton(rank, unit, 1)
                            ratio(rank, unit, behind, 1)
                        else:
                            for n in range(GROUPS):
                                residual(n)
                        product(ahead, 3)
                        dve.wait_ge(part_done, b * 2 * US_PB + it * (2 * BATCH) + 2 * (ahead + 1))
                        dve.wait_ge(u_ready, planes + (plane_index(ahead, 3) + 1))
                        dve.tensor_tensor(usum[:, ahead, :], usum[:, ahead, :], h[:, ahead, 3, :], ALU.add)\
                            .then_inc(usum_ready, 1)
                        if splits:
                            rank, unit = t_args(behind, 2)
                            newton(rank, unit, 2)
                            ratio(rank, unit, behind, 2)
                        dve.wait_ge(norm_seed_ready, b * NS_PB + it * BATCH + (HEAD_LOGS + ahead + 1))
                        inverse(b * STEPS_PB + it * (BATCH * INV_STEPS) + (HEAD_STEPS + ahead * INV_STEPS),
                                LOOP + order.index(("S", ahead, 0)), SLOTS, ahead, EPS * H_SCALE)

                iterations(dve, iteration)

                for g in range(GROUPS):
                    normalise(1, g)
                for n in range(GROUPS, PLANES):
                    residual(n)
                n_plane = lambda i, g: r_even[:, i, g, 0:SLOTS, 1:1 + W]
                centre(TAIL_MEANS, SLOTS, b * SUMS_PB + HEAD_SUMS, lambda i, g: rows(h[:, i, g, :]), n_plane)
                scale_to_unit(TAIL + BATCH, SLOTS, (b + 1) * NS_PB - BATCH, (b + 1) * STEPS_PB - BATCH * LN_STEPS,
                              LN2_EPS, n_plane)

            batches(dve, batch)

            def tiles(m, t, k):
                dve.wait_ge(out_stored, PRIMED_DMA + 16 * 2 * k)
                for e in range(2):
                    dve.wait_ge(mlp_done, PRIMED + 2 * k + (e + 1))
                    dve.wait_ge(mlp_y_in[e], 16 * k + 16)
                    dve.scalar_tensor_tensor(m_out[:, e, :], ps[0:C, BANK * (2 * HT + e):BANK * (2 * HT + e) + MT], b2_sb[:, 0:1], m_y[:, e, :],
                                             ALU.add, ALU.add).then_inc(out_ready, 1)

            mlp_loop(dve, tiles)


_INS = ["x", "L0_conv_ln1_w", "L0_conv_ln1_b", "L0_conv_w_nnmf", "L0_conv_ln2_w", "L0_conv_ln2_b",
        "L0_conv_w1", "L0_conv_b1", "L0_conv_w2", "L0_conv_b2"]


def kernel(**inputs):
    import numpy as _np
    import concourse.bacc as _bacc
    from concourse import mybir as _mybir
    from concourse.bass_utils import run_bass_kernel_spmd as _run

    nc = _bacc.Bacc("TRN2", target_bir_lowering=False, num_devices=1)
    arrays, args = {}, []
    for name in _INS:
        a = _np.ascontiguousarray(inputs[name])
        arrays[f"in_{name}_dram"] = a
        args.append(nc.dram_tensor(f"in_{name}_dram", a.shape, _mybir.dt.from_np(a.dtype), kind="ExternalInput").ap())
    args.append(nc.dram_tensor("out_dram", (N_IMG, C, H, W), _mybir.dt.float32, kind="ExternalOutput").ap())
    build_nnmf_block(nc, *args)
    r = _run(nc, [arrays], core_ids=[0])
    return r.results[0]["out_dram"]
```

```python
import numpy as np
import concourse.bass as bass
from concourse import mybir
from contextlib import ExitStack

N_IMG, C, H, W = 8, 96, 56, 56
GROUPS = 4
CG = C // GROUPS
HID = 384
N_ITER = 25
EPS = 1e-12
LN1_EPS = 1e-6
LN2_EPS = 1e-5
Q = 32
SLOTS = H // 4
WP = W + 2
R_SLOTS = SLOTS + 1
BANK = 512
PLANE, R_PLANE = SLOTS * W, R_SLOTS * W
SPLIT = 7
WP16 = W + 4
H_SCALE, W_SCALE = 2.0 ** 15, 2.0 ** 15
R_SCALE = H_SCALE * W_SCALE
BATCH = 2
SQUARES = 3
N_BATCH = N_IMG // BATCH
PLANES = BATCH * GROUPS
PAIRS = 4

ORDER = [("C", 0, 0), ("C", 0, 1), ("T", 1, 0), ("C", 0, 2), ("T", 1, 1), ("C", 0, 3), ("T", 1, 2), ("S", 0, 0),
         ("T", 1, 3),
         ("C", 1, 0), ("C", 1, 1), ("T", 0, 0), ("C", 1, 2), ("T", 0, 1), ("C", 1, 3), ("T", 0, 2), ("S", 1, 0),
         ("T", 0, 3)]
LAST_ORDER = [step for step in ORDER if step[:2] != ("T", 0)]
CONVS = [step for step in ORDER if step[0] != "S"]
assert len(CONVS) % PAIRS == 0
PAIR = {step: n % PAIRS for n, step in enumerate(CONVS)}
PAIR.update({("S", image, 0): PAIR["C", image, GROUPS - 1] for image in range(BATCH)})
assert all(PAIR["S", image, 0] == PAIR["C", 1 - image, 1] for image in range(BATCH))


def plane_index(image, g):
    return image * GROUPS + g


def build_nnmf_block(nc, x, ln1_w, ln1_b, w_nnmf, ln2_w, ln2_b, w1, b1, w2, b2, out):
    f32 = mybir.dt.float32
    ALU = mybir.AluOpType
    ACT = mybir.ActivationFunctionType
    AX = mybir.AxisListType

    y_dram = nc.dram_tensor("y_scratch", (N_IMG, C, H, W), f32, kind="Internal").ap()
    n_dram = nc.dram_tensor("n_scratch", (N_IMG, C, H, W), f32, kind="Internal").ap()

    def row_quads(t):
        return t.rearrange("n (g c) (k j) w -> n g j c k w", g=GROUPS, j=4)

    f16 = mybir.dt.float16
    h_first = H_SCALE / C
    h_first_hi = float(np.float16(h_first))
    h_first_lo = float(np.float16(h_first - h_first_hi))

    x_q, y_q, n_q = row_quads(x), row_quads(y_dram), row_quads(n_dram)

    with ExitStack() as ctx:
        def sb(name, shape, dt=f32):
            return ctx.enter_context(nc.sbuf_tensor(name, shape, dt))

        def sem(name):
            return ctx.enter_context(nc.semaphore(name))

        xn = sb("xn", [128, BATCH, GROUPS, R_PLANE])
        x_res = sb("x_res", [128, 2, PLANE])
        h = sb("h", [128, BATCH, GROUPS, PLANE])
        h_even = sb("h_even", [128, BATCH, GROUPS, 2, R_SLOTS, WP16], f16)
        h_odd = sb("h_odd", [128, BATCH, GROUPS, 2, R_SLOTS, WP16], f16)
        r_even = sb("r_even", [128, BATCH, GROUPS, R_SLOTS, WP])
        r_odd = sb("r_odd", [128, BATCH, GROUPS, SLOTS, WP])
        seed = sb("seed", [128, 2, R_PLANE])
        xseed = sb("xseed", [128, 2, R_PLANE])
        usum = sb("usum", [128, BATCH, PLANE])
        norm = sb("norm", [128, BATCH, R_PLANE])
        wt_t = sb("wt_t", [128, 2, GROUPS, 3, 2, Q], f16)
        wt_c = sb("wt_c", [128, GROUPS, 3, 2, Q])
        negones = sb("negones", [128, 128])
        ln_par = sb("ln_par", [128, 4, GROUPS])
        w1_sb = sb("w1_sb", [C, HID])
        w2_sb = sb("w2_sb", [128, HID // 128, C])
        b1_sb = sb("b1_sb", [128, HID // 128])
        b2_sb = sb("b2_sb", [C, 1])
        GUARDS = (EPS * R_SCALE, EPS * H_SCALE, EPS, LN1_EPS, LN2_EPS)
        G_R, G_H, G_X, G_LN1, G_LN2 = range(5)
        guard = sb("guard", [128, len(GUARDS)])
        ps = ctx.enter_context(nc.psum_tensor("ps", [128, 8 * BANK], f32))

        w_raw = seed[:, 0, 0:CG * 9]
        w_abs = seed[:, 0, CG * 9:2 * CG * 9]
        w_nrm = seed[:, 1, 0:9 * Q]
        w_tr = seed[:, 1, 9 * Q:18 * Q]
        w_hi = xseed[:, 0, 0:9 * Q // 2].bitcast(f16)
        w_lo = xseed[:, 1, 0:9 * Q // 2].bitcast(f16)
        w_sum = norm[:, 0, 0:1]
        w_inv = norm[:, 1, 0:1]

        MT_ROWS = 8
        MT = MT_ROWS * W
        xn_flat = xn[:, :, :, :].rearrange("p a g c -> p (a g c)")
        HT = HID // 128

        def carve(start, parts, count):
            return xn_flat[0:parts, start:start + count * MT].rearrange("p (n c) -> p n c", n=count)

        def hidden_bank(e, c):
            return ps[:, BANK * (HT * e + c):BANK * (HT * e + c) + MT]

        def out_bank(e):
            return ps[0:C, BANK * (2 * HT + e):BANK * (2 * HT + e) + MT]

        m_n, m_y = carve(0, C, 2), carve(2 * MT, C, 2)
        m_hid, m_out = carve(4 * MT, 128, 2 * HT), carve((4 + 2 * HT) * MT, C, 2)

        usum_flat = usum[:, :, :].rearrange("p i c -> p (i c)")

        def square_place(image, g, slots):
            n = plane_index(image, g) % SQUARES
            return rows(xseed[:, n, 0:slots * W] if n < 2 else usum_flat[:, 0:slots * W])

        def rows(ap):
            return ap.rearrange("p (s w) -> p s w", w=W)

        def xn_plane(image, g):
            return rows(xn[:, image, g, :])

        def n_plane(image, g):
            return r_even[:, image, g, 0:SLOTS, 1:1 + W]

        def pair_slots(pair, slots):
            start = 2 * BANK * pair + BANK - W * (slots - SPLIT)
            return rows(ps[:, start:start + W * slots])

        def halves(slots):
            return (0, slots - SPLIT), (slots - SPLIT, slots)

        w_cleared = sem("w_cleared")
        ones_set = sem("ones_set")
        w_in = sem("w_in")
        params_in = sem("params_in")
        buffers_cleared = sem("buffers_cleared")
        weight_step = sem("weight_step")
        weights_ready = sem("weights_ready")
        xn_in = sem("xn_in")
        x_res_in = [sem("x_res_in0"), sem("x_res_in1"), sem("x_res_in2")]
        y_stored = sem("y_stored")
        n_stored = sem("n_stored")
        x_mean_done = sem("x_mean_done")
        x_sum_done = sem("x_sum_done")
        y_mean_done = sem("y_mean_done")
        centered = sem("centered")
        squared = sem("squared")
        square_summed = sem("square_summed")
        scaled = sem("scaled")
        affine_done = sem("affine_done")
        x_scaled = sem("x_scaled")
        x_ready = sem("x_ready")
        recon_done = sem("recon_done")
        conv_done = sem("conv_done")
        chan_done = sem("chan_done")
        log_done = sem("log_done")
        seed_ready = sem("seed_ready")
        norm_seed_ready = sem("norm_seed_ready")
        norm_step = sem("norm_step")
        xseed_ready = sem("xseed_ready")
        prod_done = sem("prod_done")
        hi_ready = sem("hi_ready")
        lo_ready = sem("lo_ready")
        h_set = sem("h_set")
        h_filled = sem("h_filled")
        first_set = sem("first_set")
        ratio_ready = sem("ratio_ready")
        ratio_both = sem("ratio_both")
        u_ready = sem("u_ready")
        part_done = sem("part_done")
        usum_ready = sem("usum_ready")
        h_ready = sem("h_ready")
        h_both = sem("h_both")
        y_ready = sem("y_ready")
        mlp_n_in = [sem("mlp_n_in0"), sem("mlp_n_in1")]
        mlp_y_in = [sem("mlp_y_in0"), sem("mlp_y_in1")]
        hidden_done = sem("hidden_done")
        gelu_done = sem("gelu_done")
        mlp_done = sem("mlp_done")
        out_ready = sem("out_ready")
        out_stored = sem("out_stored")

        block = ctx.enter_context(nc.Block())

        PLANES_PB = N_ITER * PLANES
        HI_PB = PLANES_PB - GROUPS
        H_PB = PLANES_PB + GROUPS
        US_PB = N_ITER * BATCH
        LNS = 2 * BATCH
        LN_PLANES_PB = LNS * GROUPS
        HEAD_LOGS = 2 * BATCH
        LOGS_IT = PLANES + BATCH
        LOGS_PB = HEAD_LOGS + N_ITER * LOGS_IT + BATCH
        NS_PB = HEAD_LOGS + N_ITER * BATCH + BATCH
        LN_STEPS, INV_STEPS = 3, 2
        HEAD_STEPS = BATCH * (LN_STEPS + INV_STEPS)
        STEPS_PB = HEAD_STEPS + N_ITER * BATCH * INV_STEPS + BATCH * LN_STEPS
        WEIGHT_STEPS = 8
        N_PARAM_DMA = 4 * 4 + 4
        LOAD = 16 * 4 * PLANES
        PRIMED, PRIMED_DMA = 1, 16

        FIRST_T = (3, 0, 2, PAIR["T", 0, GROUPS - 1])
        X_MEANS, X_VARIANCES, X_SUMS = (2, 3), (0, 1), (0, 1)
        Y_MEANS, Y_VARIANCES = (2, 3), (0, 1)

        def residual_plane(n):
            if n < GROUPS:
                return r_odd[:, 0, n, :, 1:1 + W], 0
            if n < GROUPS + 2:
                return rows(x_res[:, n - GROUPS, :]), 1
            return r_odd[:, 1, n - GROUPS - 2, :, 1:1 + W], 2

        RESIDUAL_PLANES = (GROUPS, 2, 2)

        def t_rank(image, g):
            return plane_index(image, g) + (PLANES if image == 0 else 0)

        def iterations(eng, body):
            with eng.Fori(0, N_ITER - 1) as it:
                body(it, ORDER)
            body(N_ITER - 1, LAST_ORDER)

        def batches(eng, body):
            with eng.Fori(0, N_BATCH - 1) as b:
                body(b, False)
            body(N_BATCH - 1, True)

        MLP_PAIRS, MLP_TILES = N_IMG // 2, H // MT_ROWS

        def mlp_loop(eng, body):
            with eng.Fori(0, MLP_PAIRS) as m:
                with eng.Fori(0, MLP_TILES) as t:
                    body(m, t, m * MLP_TILES + t)

        def mlp_tiles(t):
            return t.rearrange("(m e) c (t r) w -> m e t c r w", e=2, r=MT_ROWS)

        @block.sync
        def _(sp):
            sp.sem_inc(y_stored, PRIMED_DMA)
            sp.sem_inc(n_stored, PRIMED_DMA)
            sp.wait_ge(w_cleared, 1)
            for g in range(GROUPS):
                sp.dma_start(w_raw[Q * g:Q * g + CG, :],
                             w_nnmf[CG * g:CG * (g + 1)].rearrange("o i a b -> o (i a b)")).then_inc(w_in, 16)

            def load_x(b):
                for image in range(BATCH):
                    for g in range(GROUPS):
                        for j in range(4):
                            q = (j + 1) % 4
                            first = 1 if q == 0 else 0
                            sp.dma_start(rows(xn[Q * q:Q * q + CG, image, g, :])[:, first:first + SLOTS, :],
                                         x_q[b * BATCH + image, g, j]).then_inc(xn_in, 16)

            def load_residual(b, n):
                image, g = divmod(n, GROUPS)
                place, group = residual_plane(n)
                for j in range(4):
                    sp.dma_start(place[Q * j:Q * j + CG], x_q[b * BATCH + image, g, j])\
                        .then_inc(x_res_in[group], 16)

            sp.wait_ge(buffers_cleared, 1)
            load_x(0)
            sp.wait_ge(buffers_cleared, 2)
            for n, par in enumerate((ln1_w, ln1_b, ln2_w, ln2_b)):
                for j in range(4):
                    sp.dma_start(ln_par[Q * j:Q * j + CG, n, :], par.rearrange("(g c) -> c g", c=CG),
                                 allow_slow_non_contiguous=True).then_inc(params_in, 16)
            sp.dma_start(w1_sb[:, :], w1[:, :]).then_inc(params_in, 16)
            sp.dma_start(w2_sb[:, :, :], w2.rearrange("(t p) c -> p t c", p=128)).then_inc(params_in, 16)
            sp.dma_start(b1_sb[:, :], b1.rearrange("(t p) -> p t", p=128),
                         allow_slow_non_contiguous=True).then_inc(params_in, 16)
            sp.dma_start(b2_sb[:, :], b2.rearrange("(c o) -> c o", o=1)).then_inc(params_in, 16)

            def batch(b, last):
                load_residual(b, GROUPS)
                load_residual(b, GROUPS + 1)
                for n in range(GROUPS):
                    sp.wait_ge(conv_done, b * PLANES_PB + ((N_ITER - 1) * PLANES + n + 1))
                    load_residual(b, n)
                for n in range(2):
                    sp.wait_ge(conv_done, b * PLANES_PB + ((N_ITER - 1) * PLANES + GROUPS + n + 1))
                    load_residual(b, GROUPS + 2 + n)
                if not last:
                    sp.wait_ge(ratio_ready, (b + 1) * PLANES_PB)
                    load_x(b + 1)
                for n in range(PLANES):
                    image, g = divmod(n, GROUPS)
                    sp.wait_ge(y_ready, b * PLANES + n + 1)
                    for j in range(4):
                        sp.dma_start(y_q[b * BATCH + image, g, j], rows(h[Q * j:Q * j + CG, image, g, :]))\
                            .then_inc(y_stored, 16)
                if not last:
                    for image in range(BATCH):
                        store_n(b, image)

            def store_n(b, image):
                for g in range(GROUPS):
                    sp.wait_ge(affine_done, b * LN_PLANES_PB + PLANES + plane_index(image, g) + 1)
                    for j in range(4):
                        sp.dma_start(n_q[b * BATCH + image, g, j],
                                     r_even[Q * j:Q * j + CG, image, g, 0:SLOTS, 1:1 + W]).then_inc(n_stored, 16)

            batches(sp, batch)

            n_t, y_t = mlp_tiles(n_dram), mlp_tiles(y_dram)

            def load_tiles(m, t):
                k = m * MLP_TILES + t
                sp.wait_ge(hidden_done, PRIMED + 2 * k)
                for e in range(2):
                    sp.dma_start(m_n[:, e, :].rearrange("p (r w) -> p r w", w=W), n_t[m, e, t])\
                        .then_inc(mlp_n_in[e], 16)
                sp.wait_ge(out_ready, PRIMED + 2 * k)
                for e in range(2):
                    sp.dma_start(m_y[:, e, :].rearrange("p (r w) -> p r w", w=W), y_t[m, e, t])\
                        .then_inc(mlp_y_in[e], 16)

            for m in range(MLP_PAIRS):
                if m == 0:
                    sp.wait_ge(y_stored, PRIMED_DMA + LOAD)
                    sp.wait_ge(n_stored, PRIMED_DMA + LOAD)
                    for image in range(BATCH):
                        load_tiles(0, image)
                        store_n(N_BATCH - 1, image)
                else:
                    sp.wait_ge(y_stored, PRIMED_DMA + (m + 1) * LOAD)
                    sp.wait_ge(n_stored, PRIMED_DMA + (m + 1) * LOAD)
                with sp.Fori(BATCH if m == 0 else 0, MLP_TILES) as t:
                    load_tiles(m, t)

            sp.wait_ge(out_stored, PRIMED_DMA + 16 * 2 * MLP_PAIRS * MLP_TILES)

        @block.gpsimd
        def _(pool):
            pool.memset(xn[:, :, :, :], 0.0)
            pool.memset(x_res[:, :, :], 0.0).then_inc(buffers_cleared, 1)
            pool.memset(wt_t[:, :, :, :, :, :], 0.0)
            pool.memset(wt_c[:, :, :, :, :], 0.0)
            pool.memset(ln_par[:, :, :], 0.0).then_inc(buffers_cleared, 1)
            for n, eps in enumerate(GUARDS):
                pool.memset(guard[:, n:n + 1], eps)
            pool.memset(h_even[:, :, :, :, :, :].bitcast(f32), 0.0)
            pool.memset(h_odd[:, :, :, :, :, :].bitcast(f32), 0.0).then_inc(buffers_cleared, 1)

            def first_h():
                pool.memset(h_even[:, 0, :, 0, 0:SLOTS, 2:2 + W], h_first_hi)
                pool.memset(h_even[:, 0, :, 1, 0:SLOTS, 2:2 + W], h_first_lo)
                pool.memset(h_odd[:, 0, :, 0, 1:SLOTS, 2:2 + W], h_first_hi)
                pool.memset(h_odd[:, 0, :, 1, 1:SLOTS, 2:2 + W], h_first_lo).then_inc(h_set, 1)

            pool.wait_ge(buffers_cleared, 3)
            first_h()

            def xseed_plane(rank, image, g, first=False):
                pool.wait_ge(seed_ready, rank + 1)
                if not first:
                    pool.wait_ge(ratio_ready, rank - 1)
                pool.tensor_tensor(xseed[:, g % 2, :], xn[:, image, g, :], seed[:, g % 2, :], ALU.mult)\
                    .then_inc(xseed_ready, 1)

            def batch(b, last):
                pool.wait_ge(x_ready, b * PLANES + GROUPS)
                xseed_plane(b * PLANES_PB, 0, 0, True)
                pool.memset(h[:, 1, :, :], 1.0)
                xseed_plane(b * PLANES_PB + 1, 0, 1, True)
                pool.memset(h[:, 0, :, :], h_first).then_inc(h_filled, 1)
                xseed_plane(b * PLANES_PB + 2, 0, 2)
                pool.wait_ge(x_ready, (b + 1) * PLANES)
                xseed_plane(b * PLANES_PB + 3, 0, 3)

                def iteration(it, order):
                    planes = b * PLANES_PB + it * PLANES
                    for what, image, g in order:
                        if what == "T":
                            xseed_plane(planes + t_rank(image, g), image, g)
                        elif what == "C" and g == 1:
                            pool.wait_ge(u_ready, planes + (plane_index(image, g) + 1))
                            pool.tensor_tensor(usum[:, image, :], h[:, image, 0, :], h[:, image, 1, :], ALU.add)\
                                .then_inc(part_done, 1)
                        elif what == "C" and g == 2:
                            parts = b * 2 * US_PB + it * (2 * BATCH) + 2 * image
                            pool.wait_ge(u_ready, planes + (plane_index(image, g) + 1))
                            pool.wait_ge(part_done, parts + 1)
                            pool.tensor_tensor(usum[:, image, :], usum[:, image, :], h[:, image, 2, :], ALU.add)\
                                .then_inc(part_done, 1)

                iterations(pool, iteration)
                if not last:
                    first_h()

            batches(pool, batch)

        @block.tensor
        def _(pe):
            for primed in (hidden_done, mlp_done):
                pe.sem_inc(primed, PRIMED)
            pe.wait_ge(ones_set, 5)

            def pair_free(b, it, step):
                planes = b * PLANES_PB + it * PLANES
                if step[0] == "S":
                    return
                if step[0] == "C" and step[2] == 1:
                    pe.wait_ge(norm_step, b * STEPS_PB + it * (BATCH * INV_STEPS)
                               + (HEAD_STEPS + step[1] * INV_STEPS))
                    return
                n = CONVS.index(step)
                earlier = PLANES if n < PAIRS else 0
                what, image, g = CONVS[n - PAIRS]
                if what == "T":
                    pe.wait_ge(ratio_ready, planes + (t_rank(image, g) + 1 - earlier))
                else:
                    pe.wait_ge(u_ready, planes + (plane_index(image, g) + 1 - earlier))

            def bank_part(pair, slots, half):
                a, e = halves(slots)[half]
                return pair_slots(pair, slots)[:, a:e, :], a, e

            def ones_sum(pair, slots, srcs, after_each=None, before_each=None):
                for n, src in enumerate(srcs):
                    if before_each:
                        before_each(n)
                    for half in range(2):
                        dst, a, e = bank_part(pair, slots, half)
                        last = pe.matmul(dst, negones[:, :], src[:, a:e, :], start=n == 0, stop=n == len(srcs) - 1,
                                         skip_group_check=True)
                    if after_each:
                        last.then_inc(after_each, 1)
                return last

            def transposed_conv(pair, image, g):
                for half in range(2):
                    dst, a, e = bank_part(pair, R_SLOTS, half)
                    for kx in range(3):
                        col = 1 + 2 - kx
                        for part, (w_part, h_part) in enumerate(((0, 0), (1, 0), (0, 1))):
                            for tile, src in ((0, h_odd), (64, h_even)):
                                last = pe.matmul(dst[tile:tile + 64], wt_t[:, w_part, g, kx, :, :]
                                                 .rearrange("p a b -> p (a b)"),
                                                 src[:, image, g, h_part, a:e, col:col + W],
                                                 start=kx == 0 and part == 0, stop=kx == 2 and part == 2,
                                                 skip_group_check=True)
                return last

            def conv(pair, image, g):
                for half in range(2):
                    dst, a, e = bank_part(pair, SLOTS, half)
                    for kx in range(3):
                        for tile, src in ((0, r_even), (64, r_odd)):
                            last = pe.matmul(dst[tile:tile + 64], wt_c[:, g, kx, :, :].rearrange("p a b -> p (a b)"),
                                             src[:, image, g, a:e, kx:kx + W],
                                             start=kx == 0, stop=kx == 2, skip_group_check=True)
                return last

            def mean(pair, slots, src, before_each, signal):
                ones_sum(pair, slots, [src(g) for g in range(GROUPS)], before_each=before_each).then_inc(signal, 1)

            def x_mean(b, image):
                mean(X_MEANS[image], R_SLOTS, lambda g: rows(xn[:, image, g, :]), None, x_mean_done)

            def y_mean(b, image):
                mean(Y_MEANS[image], SLOTS, lambda g: rows(h[:, image, g, :]),
                     lambda g: pe.wait_ge(y_ready, b * PLANES + (image * GROUPS + g + 1)), y_mean_done)

            def variance(b, pairs, slots, ln, image):
                n = b * LN_PLANES_PB + (ln + image) * GROUPS
                ones_sum(pairs[image], slots, [square_place(image, g, slots) for g in range(GROUPS)],
                         after_each=square_summed, before_each=lambda g: pe.wait_ge(squared, n + g + 1))

            pe.wait_ge(xn_in, LOAD)
            for image in range(BATCH):
                x_mean(0, image)

            def batch(b, last):
                for image in range(BATCH):
                    variance(b, X_VARIANCES, R_SLOTS, 0, image)

                def first_t(g):
                    pe.wait_ge(h_both, b * PLANES_PB + (g + 1))
                    transposed_conv(FIRST_T[g], 0, g).then_inc(recon_done, 1)

                pe.wait_ge(weights_ready, 1)
                first_t(0)
                for image in range(BATCH):
                    n = b * LN_PLANES_PB + image * GROUPS
                    ones_sum(X_SUMS[image], R_SLOTS, [rows(xn[:, image, g, :]) for g in range(GROUPS)],
                             before_each=lambda g: pe.wait_ge(affine_done, n + g + 1)).then_inc(x_sum_done, 1)
                pe.wait_ge(norm_step, b * STEPS_PB + (HEAD_STEPS - INV_STEPS))
                first_t(1)
                first_t(2)
                pe.wait_ge(ratio_ready, b * PLANES_PB + 1)
                first_t(3)

                def iteration(it, order):
                    planes = b * PLANES_PB + it * PLANES
                    for what, image, g in order:
                        if order is LAST_ORDER and (what, image) == ("S", 1):
                            y_mean(b, 0)
                        pair_free(b, it, (what, image, g))
                        pair = PAIR[what, image, g]
                        if what == "T":
                            pe.wait_ge(h_both, planes + (t_rank(image, g) + 1))
                            transposed_conv(pair, image, g).then_inc(recon_done, 1)
                        elif what == "C":
                            pe.wait_ge(ratio_both, planes + (plane_index(image, g) + 1))
                            conv(pair, image, g).then_inc(conv_done, 1)
                        else:
                            pe.wait_ge(usum_ready, b * US_PB + it * BATCH + (image + 1))
                            ones_sum(pair, SLOTS, [rows(usum[:, image, :])]).then_inc(chan_done, 1)

                iterations(pe, iteration)

                variance(b, Y_VARIANCES, SLOTS, BATCH, 0)
                y_mean(b, 1)
                if not last:
                    pe.wait_ge(xn_in, (b + 2) * LOAD)
                    x_mean(b + 1, 0)
                variance(b, Y_VARIANCES, SLOTS, BATCH, 1)
                if not last:
                    x_mean(b + 1, 1)

            batches(pe, batch)

            pe.wait_ge(scaled, PRIMED + N_BATCH * LN_PLANES_PB)

            def tiles(m, t, k):
                for e in range(2):
                    pe.wait_ge(mlp_n_in[e], 16 * k + 16)
                    for c in range(HT):
                        last = pe.matmul(hidden_bank(e, c), w1_sb[:, 128 * c:128 * (c + 1)], m_n[:, e, :],
                                         start=True, stop=True)
                    last.then_inc(hidden_done, 1)
                pe.wait_ge(out_ready, PRIMED + 2 * k)
                for e in range(2):
                    pe.wait_ge(gelu_done, 2 * k + (e + 1))
                    for c in range(HT):
                        last = pe.matmul(out_bank(e), w2_sb[:, c, :], m_hid[:, HT * e + c, :],
                                         start=c == 0, stop=c == HT - 1)
                    last.then_inc(mlp_done, 1)

            mlp_loop(pe, tiles)

        @block.scalar
        def _(act):
            act.sem_inc(out_stored, PRIMED_DMA)
            act.preload_act_table_set("natural_log_exp_and_others")
            act.wait_ge(weight_step, WEIGHT_STEPS)
            act.wait_ge(buffers_cleared, 3)
            for ky in range(3):
                for row in range(2):
                    for g in range(GROUPS):
                        def spread(dst, src, q):
                            return act.activation(
                                dst[Q * q:Q * (q + 1), g, :, row, :],
                                src[Q * g:Q * (g + 1), 3 * Q * ky:3 * Q * (ky + 1)]
                                .rearrange("p (k m) -> p k m", m=Q), ACT.Copy)
                        spread(wt_t[:, 0], w_hi, 1 + row + 1 - ky)
                        spread(wt_t[:, 1], w_lo, 1 + row + 1 - ky)
                        last = spread(wt_c, w_tr, 1 + row + ky - 1)
            last.then_inc(weights_ready, 1)
            act.wait_ge(params_in, 16 * N_PARAM_DMA)
            act.wait_ge(weights_ready, 1)

            def log_exp(log_count, src, dst, eps, factor, power, signal):
                act.activation(dst, src, ACT.Ln, bias=guard[:, eps:eps + 1], scale=factor).then_inc(log_done, 1)
                act.wait_ge(log_done, log_count + 1)
                act.activation(dst, dst, ACT.Exp, scale=power).then_inc(signal, 1)

            def norm_seed(log_count, pair, slots, image, eps):
                log_exp(log_count, pair_slots(pair, slots), rows(norm[:, image, 0:slots * W]), eps, -1.0, -1.0,
                        norm_seed_ready)

            def squares(b, ln, slots, image, plane):
                for g in range(GROUPS):
                    n = b * LN_PLANES_PB + (ln + image) * GROUPS + g
                    act.wait_ge(centered, n + 1)
                    if plane_index(image, g) >= SQUARES:
                        act.wait_ge(square_summed, n + 1 - SQUARES)
                    act.activation(square_place(image, g, slots), plane(image, g), ACT.Square)\
                        .then_inc(squared, 1)

            def deviation_seed(b, ln, slots, image, pairs, log_count, eps):
                act.wait_ge(square_summed, b * LN_PLANES_PB + (ln + image + 1) * GROUPS)
                log_exp(log_count + image, pair_slots(pairs[image], slots), rows(norm[:, image, 0:slots * W]), eps,
                        -1.0 / C, -0.5, norm_seed_ready)

            def affine(b, ln, image, plane, func, first_par):
                for g in range(GROUPS):
                    act.wait_ge(scaled, PRIMED + b * LN_PLANES_PB + (ln + image) * GROUPS + g + 1)
                    act.activation(plane(image, g), plane(image, g), func, scale=ln_par[:, first_par, g:g + 1],
                                   bias=ln_par[:, first_par + 1, g:g + 1]).then_inc(affine_done, 1)

            squares(0, 0, R_SLOTS, 0, xn_plane)

            def batch(b, last):
                act.wait_ge(h_set, b + 1)
                act.activation(h_odd[64:128, 0, :, :, 0, 2:2 + W], h_even[0:64, 0, :, :, 0, 2:2 + W], ACT.Copy)
                act.activation(h_odd[0:64, 0, :, :, SLOTS, 2:2 + W], h_even[64:128, 0, :, :, SLOTS - 1, 2:2 + W],
                               ACT.Copy).then_inc(h_both, GROUPS)
                deviation_seed(b, 0, R_SLOTS, 0, X_VARIANCES, b * LOGS_PB, G_LN1)
                squares(b, 0, R_SLOTS, 1, xn_plane)
                deviation_seed(b, 0, R_SLOTS, 1, X_VARIANCES, b * LOGS_PB, G_LN1)

                def seed_plane(log_count, rank, pair, g, first=False):
                    act.wait_ge(recon_done, rank + 1)
                    if not first:
                        act.wait_ge(ratio_ready, rank - 1)
                    log_exp(log_count, pair_slots(pair, R_SLOTS), rows(seed[:, g % 2, :]), G_R, -1.0, -1.0,
                            seed_ready)

                def ratio_copy(rank, image, g):
                    act.wait_ge(ratio_ready, rank + 1)
                    act.activation(r_odd[0:64, image, g, :, 1:1 + W], r_even[64:128, image, g, 0:SLOTS, 1:1 + W],
                                   ACT.Copy)
                    act.activation(r_odd[64:128, image, g, :, 1:1 + W],
                                   r_even[0:64, image, g, 1:R_SLOTS, 1:1 + W], ACT.Copy).then_inc(ratio_both, 1)

                first, logs = b * PLANES_PB, b * LOGS_PB
                affine(b, 0, 0, xn_plane, ACT.Relu, 0)
                seed_plane(logs + BATCH, first, FIRST_T[0], 0, True)
                for image in range(BATCH):
                    if image:
                        affine(b, 0, image, xn_plane, ACT.Relu, 0)
                    act.wait_ge(x_sum_done, b * BATCH + image + 1)
                    norm_seed(logs + (BATCH + 1 + image), X_SUMS[image], R_SLOTS, image, G_X)
                for g in range(1, GROUPS):
                    seed_plane(logs + (HEAD_LOGS + g), first + g, FIRST_T[g], g, g < 2)
                    ratio_copy(first + g - 1, 0, g - 1)

                def iteration(it, order):
                    planes = b * PLANES_PB + it * PLANES
                    logs = b * LOGS_PB + it * LOGS_IT + (HEAD_LOGS + GROUPS)
                    n_log = 0
                    for what, image, g in order:
                        if what == "T":
                            rank = t_rank(image, g)
                            seed_plane(logs + n_log, planes + rank, PAIR[what, image, g], g)
                            ratio_copy(planes + (rank - 1), *divmod((rank - 1) % PLANES, GROUPS))
                            n_log += 1
                        elif what == "S":
                            act.wait_ge(chan_done, b * US_PB + it * BATCH + (image + 1))
                            norm_seed(logs + n_log, PAIR[what, image, g], SLOTS, image, G_H)
                            n_log += 1
                        if order is LAST_ORDER and (what, image, g) == ("T", 1, GROUPS - 1):
                            ratio_copy(planes + rank, image, g)

                iterations(act, iteration)

                logs = (b + 1) * LOGS_PB - BATCH
                squares(b, BATCH, SLOTS, 0, n_plane)
                deviation_seed(b, BATCH, SLOTS, 0, Y_VARIANCES, logs, G_LN2)
                squares(b, BATCH, SLOTS, 1, n_plane)
                affine(b, BATCH, 0, n_plane, ACT.Identity, 2)
                deviation_seed(b, BATCH, SLOTS, 1, Y_VARIANCES, logs, G_LN2)
                if not last:
                    squares(b + 1, 0, R_SLOTS, 0, xn_plane)
                affine(b, BATCH, 1, n_plane, ACT.Identity, 2)

            batches(act, batch)
            act.preload_act_table(ACT.Gelu)

            def tiles(m, t, k):
                act.wait_ge(mlp_done, PRIMED + 2 * k)
                for e in range(2):
                    act.wait_ge(hidden_done, PRIMED + 2 * k + (e + 1))
                    for c in range(HT):
                        last = act.activation(m_hid[:, HT * e + c, :], hidden_bank(e, c), ACT.Gelu,
                                              bias=b1_sb[:, c:c + 1])
                    last.then_inc(gelu_done, 1)
                out_t = mlp_tiles(out)
                for e in range(2):
                    act.wait_ge(out_ready, PRIMED + 2 * k + (e + 1))
                    act.dma_start(out_t[m, e, t], m_out[:, e, :].rearrange("p (r w) -> p r w", w=W))\
                        .then_inc(out_stored, 16)

            mlp_loop(act, tiles)

        @block.vector
        def _(dve):
            for primed in (scaled, out_ready):
                dve.sem_inc(primed, PRIMED)
            dve.memset(seed[:, :, :], 0.0).then_inc(w_cleared, 1)
            dve.memset(negones[:, :], 0.0).then_inc(ones_set, 1)
            dve.wait_ge(ones_set, 1)
            for j in range(4):
                dve.memset(negones[Q * j:Q * j + CG, Q * j:Q * (j + 1)], -1.0).then_inc(ones_set, 1)
            dve.memset(r_even[:, :, :, :, :], 0.0)
            dve.memset(r_odd[:, :, :, :, :], 0.0)
            dve.wait_ge(buffers_cleared, 3)
            dve.wait_ge(w_in, 16 * GROUPS)
            dve.scalar_tensor_tensor(w_abs, w_raw, -1.0, w_raw, ALU.mult, ALU.max).then_inc(weight_step, 1)
            dve.wait_ge(weight_step, 1)
            dve.reduce_sum(w_sum, w_abs, AX.X).then_inc(weight_step, 1)
            dve.wait_ge(weight_step, 2)
            dve.tensor_scalar_add(w_sum, w_sum, EPS).then_inc(weight_step, 1)
            dve.wait_ge(weight_step, 3)
            dve.reciprocal(w_inv, w_sum).then_inc(weight_step, 1)
            dve.wait_ge(weight_step, 4)
            dve.tensor_scalar(w_nrm.rearrange("p (t i) -> p t i", i=Q)[:, :, 0:CG],
                              w_abs.rearrange("p (i t) -> p t i", i=CG), w_inv, None, ALU.mult)\
                .then_inc(weight_step, 1)
            dve.wait_ge(weight_step, 5)
            dve.transpose(w_tr, w_nrm).then_inc(weight_step, 1)
            dve.tensor_scalar(w_hi, w_nrm, -W_SCALE, None, ALU.mult).then_inc(weight_step, 1)
            dve.wait_ge(weight_step, 7)
            dve.scalar_tensor_tensor(w_lo, w_nrm, -W_SCALE, w_hi, ALU.mult, ALU.subtract).then_inc(weight_step, 1)

            def inverse(steps, pair, slots, image, guard_value):
                prod, seed_n = pair_slots(pair, slots), rows(norm[:, image, 0:slots * W])
                dve.scalar_tensor_tensor(prod, prod, -guard_value, seed_n, ALU.add, ALU.mult).then_inc(norm_step, 1)
                dve.wait_ge(norm_step, steps + 1)
                dve.scalar_tensor_tensor(seed_n, prod, 2.0, seed_n, ALU.add, ALU.mult).then_inc(norm_step, 1)
                dve.wait_ge(norm_step, steps + 2)

            def centre(pairs, slots, image, count, signal, src, dst):
                dve.wait_ge(signal, count + image + 1)
                for g in range(GROUPS):
                    dve.scalar_tensor_tensor(dst(image, g), pair_slots(pairs[image], slots), 1.0 / C,
                                             src(image, g), ALU.mult, ALU.add).then_inc(centered, 1)

            def scale_to_unit(pairs, slots, image, seeds, steps, eps, dst):
                y, s = (rows(t[:, image, 0:slots * W]) for t in (norm, seed))
                dve.wait_ge(norm_seed_ready, seeds + image + 1)
                dve.tensor_tensor(s, y, y, ALU.mult).then_inc(norm_step, 1)
                dve.wait_ge(norm_step, steps + image * LN_STEPS + 1)
                dve.scalar_tensor_tensor(s, pair_slots(pairs[image], slots), -C * eps, s,
                                         ALU.add, ALU.mult).then_inc(norm_step, 1)
                dve.wait_ge(norm_step, steps + image * LN_STEPS + 2)
                dve.scalar_tensor_tensor(y, s, 3.0 * C, y, ALU.add, ALU.mult).then_inc(norm_step, 1)
                dve.wait_ge(norm_step, steps + image * LN_STEPS + 3)
                for g in range(GROUPS):
                    dve.scalar_tensor_tensor(dst(image, g), dst(image, g), 0.5 / C, y,
                                             ALU.mult, ALU.mult).then_inc(scaled, 1)

            def normalise(image, g):
                dve.scalar_tensor_tensor(h[:, image, g, :], h[:, image, g, :], H_SCALE, norm[:, image, 0:PLANE],
                                         ALU.mult, ALU.mult).then_inc(h_ready, 1)

            def centre_x(b, image):
                centre(X_MEANS, R_SLOTS, image, b * BATCH, x_mean_done, xn_plane, xn_plane)

            dve.wait_ge(xn_in, LOAD)
            centre_x(0, 0)

            def batch(b, last):
                centre_x(b, 1)
                dve.wait_ge(weights_ready, 1)
                for image in range(BATCH):
                    scale_to_unit(X_VARIANCES, R_SLOTS, image, b * NS_PB, b * STEPS_PB, LN1_EPS, xn_plane)

                def inverse_x_sum(image):
                    dve.wait_ge(norm_seed_ready, b * NS_PB + (BATCH + image + 1))
                    inverse(b * STEPS_PB + (BATCH * LN_STEPS + image * INV_STEPS), X_SUMS[image], R_SLOTS, image,
                            EPS)

                def normalise_x(image):
                    for g in range(GROUPS):
                        dve.scalar_tensor_tensor(xn[:, image, g, :], xn[:, image, g, :], R_SCALE, norm[:, image, :],
                                                 ALU.mult, ALU.mult).then_inc(x_scaled, 1)
                    dve.wait_ge(x_scaled, b * PLANES + (image + 1) * GROUPS)
                    dve.memset(xn[0:Q, image, :, 0:W], 0.0)
                    dve.memset(xn[Q:2 * Q, image, :, PLANE:R_PLANE], 0.0)
                    dve.memset(xn[2 * Q:4 * Q, image, :, PLANE:R_PLANE], 0.0).then_inc(x_ready, GROUPS)

                def newton(rank, pair, g):
                    prod = pair_slots(pair, R_SLOTS)
                    dve.wait_ge(seed_ready, rank + 1)
                    dve.scalar_tensor_tensor(prod, prod, -EPS * R_SCALE, rows(seed[:, g % 2, :]),
                                             ALU.add, ALU.mult).then_inc(prod_done, 1)

                def ratio(rank, pair, image, g):
                    dve.wait_ge(prod_done, rank + 1)
                    dve.wait_ge(xseed_ready, rank + 1)
                    dve.scalar_tensor_tensor(r_even[:, image, g, :, 1:1 + W], pair_slots(pair, R_SLOTS), 2.0,
                                             rows(xseed[:, g % 2, :]), ALU.add, ALU.mult).then_inc(ratio_ready, 1)

                def first_ratio(g):
                    newton(b * PLANES_PB + g, FIRST_T[g], g)
                    ratio(b * PLANES_PB + g, FIRST_T[g], 0, g)

                inverse_x_sum(0)
                dve.wait_ge(y_stored, PRIMED_DMA + b * LOAD)
                dve.wait_ge(n_stored, PRIMED_DMA + b * LOAD)
                normalise_x(0)
                first_ratio(0)
                inverse_x_sum(1)
                first_ratio(1)
                dve.wait_ge(h_filled, b + 1)
                first_ratio(2)
                normalise_x(1)
                dve.memset(norm[:, 1, 0:PLANE], 1.0 / C).then_inc(first_set, 1)
                def residual(n):
                    image, g = divmod(n, GROUPS)
                    dve.wait_ge(h_ready, b * H_PB + (N_ITER * PLANES - GROUPS + n + 1))
                    place, group = residual_plane(n)
                    dve.wait_ge(x_res_in[group], (b + 1) * (16 * 4 * RESIDUAL_PLANES[group]))
                    dve.scalar_tensor_tensor(rows(h[:, image, g, :]), rows(h[:, image, g, :]), 1.0 / H_SCALE, place,
                                             ALU.mult, ALU.add).then_inc(y_ready, 1)

                def centre_y(image):
                    centre(Y_MEANS, SLOTS, image, b * BATCH, y_mean_done, lambda i, g: rows(h[:, i, g, :]), n_plane)

                def iteration(it, order):
                    planes = b * PLANES_PB + it * PLANES
                    last_iteration = order is LAST_ORDER

                    def split(image, g):
                        n = b * HI_PB + it * PLANES + ((1 - image) * GROUPS + g + 1)
                        high, low = (h_even[:, image, g, part, 0:SLOTS, 2:2 + W] for part in range(2))
                        dve.wait_ge(h_ready, b * H_PB + it * PLANES + ((1 - image) * GROUPS + g + 1))
                        dve.tensor_copy(high, rows(h[:, image, g, :])).then_inc(hi_ready, 1)
                        dve.wait_ge(hi_ready, n)
                        dve.tensor_tensor(low, rows(h[:, image, g, :]), high, ALU.subtract).then_inc(lo_ready, 1)
                        dve.wait_ge(lo_ready, n)
                        dve.tensor_copy(h_odd[64:128, image, g, :, 0:SLOTS, 2:2 + W],
                                        h_even[0:64, image, g, :, 0:SLOTS, 2:2 + W])
                        dve.tensor_copy(h_odd[0:64, image, g, :, 1:SLOTS + 1, 2:2 + W],
                                        h_even[64:128, image, g, :, 0:SLOTS, 2:2 + W]).then_inc(h_both, 1)

                    def product(image, g):
                        dve.wait_ge(conv_done, planes + (plane_index(image, g) + 1))
                        dve.tensor_tensor(rows(h[:, image, g, :]), rows(h[:, image, g, :]),
                                          pair_slots(PAIR["C", image, g], SLOTS), ALU.mult)\
                            .then_inc(u_ready, 1)

                    for ahead in range(BATCH):
                        behind = 1 - ahead
                        splits = not (last_iteration and behind == 0)

                        def new_t(g):
                            return planes + t_rank(behind, g), PAIR["T", behind, g]

                        if ahead == 0:
                            dve.wait_ge(first_set, b + 1)
                        normalise(behind, 0)
                        if splits:
                            split(behind, 0)
                        rank = planes + plane_index(ahead, GROUPS - 1)
                        pair = PAIR["T", ahead, GROUPS - 1]
                        newton(rank, pair, GROUPS - 1)
                        ratio(rank, pair, ahead, GROUPS - 1)
                        product(ahead, 0)
                        normalise(behind, 1)
                        if splits:
                            split(behind, 1)
                        product(ahead, 1)
                        normalise(behind, 2)
                        if splits:
                            split(behind, 2)
                            newton(*new_t(0), 0)
                        normalise(behind, 3)
                        if splits:
                            ratio(*new_t(0), behind, 0)
                        else:
                            residual(0)
                            residual(1)
                        product(ahead, 2)
                        if splits:
                            split(behind, 3)
                            newton(*new_t(1), 1)
                            ratio(*new_t(1), behind, 1)
                        else:
                            residual(2)
                            residual(3)
                        product(ahead, 3)
                        dve.wait_ge(part_done, b * 2 * US_PB + it * (2 * BATCH) + 2 * (ahead + 1))
                        dve.wait_ge(u_ready, planes + (plane_index(ahead, 3) + 1))
                        dve.tensor_tensor(usum[:, ahead, :], usum[:, ahead, :], h[:, ahead, 3, :], ALU.add)\
                            .then_inc(usum_ready, 1)
                        if splits:
                            newton(*new_t(2), 2)
                            ratio(*new_t(2), behind, 2)
                        else:
                            centre_y(0)
                        dve.wait_ge(norm_seed_ready, b * NS_PB + it * BATCH + (HEAD_LOGS + ahead + 1))
                        inverse(b * STEPS_PB + it * (BATCH * INV_STEPS) + (HEAD_STEPS + ahead * INV_STEPS),
                                PAIR["S", ahead, 0], SLOTS, ahead, EPS * H_SCALE)

                iterations(dve, iteration)

                normalise(1, 0)
                for g in range(1, GROUPS):
                    normalise(1, g)
                    residual(GROUPS + g - 1)
                residual(PLANES - 1)
                centre_y(1)
                for image in range(BATCH):
                    if image and not last:
                        dve.wait_ge(xn_in, (b + 2) * LOAD)
                        centre_x(b + 1, 0)
                    scale_to_unit(Y_VARIANCES, SLOTS, image, (b + 1) * NS_PB - BATCH,
                                  (b + 1) * STEPS_PB - BATCH * LN_STEPS, LN2_EPS, n_plane)

            batches(dve, batch)

            def tiles(m, t, k):
                dve.wait_ge(out_stored, PRIMED_DMA + 16 * 2 * k)
                for e in range(2):
                    dve.wait_ge(mlp_done, PRIMED + 2 * k + (e + 1))
                    dve.wait_ge(mlp_y_in[e], 16 * k + 16)
                    dve.scalar_tensor_tensor(m_out[:, e, :], out_bank(e), b2_sb[:, 0:1], m_y[:, e, :],
                                             ALU.add, ALU.add).then_inc(out_ready, 1)

            mlp_loop(dve, tiles)


_INS = ["x", "L0_conv_ln1_w", "L0_conv_ln1_b", "L0_conv_w_nnmf", "L0_conv_ln2_w", "L0_conv_ln2_b",
        "L0_conv_w1", "L0_conv_b1", "L0_conv_w2", "L0_conv_b2"]


def kernel(**inputs):
    import numpy as _np
    import concourse.bacc as _bacc
    from concourse import mybir as _mybir
    from concourse.bass_utils import run_bass_kernel_spmd as _run

    nc = _bacc.Bacc("TRN2", target_bir_lowering=False, num_devices=1)
    arrays, args = {}, []
    for name in _INS:
        a = _np.ascontiguousarray(inputs[name])
        arrays[f"in_{name}_dram"] = a
        args.append(nc.dram_tensor(f"in_{name}_dram", a.shape, _mybir.dt.from_np(a.dtype), kind="ExternalInput").ap())
    args.append(nc.dram_tensor("out_dram", (N_IMG, C, H, W), _mybir.dt.float32, kind="ExternalOutput").ap())
    build_nnmf_block(nc, *args)
    r = _run(nc, [arrays], core_ids=[0])
    return r.results[0]["out_dram"]
```
